# Optimizing a Trainium2 kernel written in Bass

```python
import numpy as np
import jax
import jax.numpy as jnp

def _softmax(x, axis=-1):
    return jax.nn.softmax(x, axis=axis)

def _gelu(x):
    return jax.nn.gelu(x, approximate=True)

def _silu(x):
    return jax.nn.silu(x)

def _sigmoid(x):
    return jax.nn.sigmoid(x)

def _layernorm(x, axis=-1, eps=1e-05):
    m = jnp.mean(x, axis=axis, keepdims=True)
    v = jnp.var(x, axis=axis, keepdims=True)
    return (x - m) / jnp.sqrt(v + eps)

def _scatter_add(tgt, idx, src, axis=0):
    return tgt.at[idx].add(src)

def _segment_sum(src, seg, n):
    return jax.ops.segment_sum(src, seg, n)
kernel_name = 'mk_xattn_seq_d4_seqx_r8_d42e36'

def setup_inputs(seed: int=0):
    np.random.seed(seed)
    _w = jnp.asarray

    def _rec_inputs():
        import jax
        import jax.numpy as jnp
        _rk = jax.random.key(seed)
        x = -0.0002928 + 1 * jax.random.normal(jax.random.fold_in(_rk, 1), (16, 128, 256), jnp.float32)
        _lenS = 128 - jax.random.randint(jax.random.fold_in(_rk, 7), (16,), 0, max(1, 128 // 4) + 1, jnp.int32)
        _lenS2 = 128 - jax.random.randint(jax.random.fold_in(_rk, 8), (16,), 0, max(1, 128 // 4) + 1, jnp.int32)
        _ctx_2048P = jax.random.normal(jax.random.fold_in(_rk, 11), (16, 16, 256), jnp.float32)
        _ctx_2048c = jax.random.dirichlet(jax.random.fold_in(_rk, 511), 0.3 * jnp.ones((16,), jnp.float32), (16, 128))
        _ctx_2048t = jnp.einsum('bsk,bkd->bsd', _ctx_2048c, _ctx_2048P)
        _ctx_2048t = _ctx_2048t * jax.lax.rsqrt(jnp.mean(jnp.square(_ctx_2048t)) + 1e-12) * 0.953939
        ctx_2048 = 0.000189249 + 0.0999589 * (_ctx_2048t + 0.3 * jax.random.normal(jax.random.fold_in(_rk, 611), (16, 128, 256), jnp.float32))
        _validS = jnp.arange(128)[None, :] < _lenS[:, None]
        _validS2 = jnp.arange(128)[None, :] < _lenS2[:, None]
        _causal = jnp.tril(jnp.ones((128, 128), dtype=bool))
        mask_BxS2_bf1 = jnp.ones((16, 128), dtype=bool)
        return (x, ctx_2048, mask_BxS2_bf1)
    x, ctx_2048, mask_BxS2_bf1 = _rec_inputs()

    def _L0_xattn_setup():
        import jax, jax.numpy as jnp
        import numpy as np
        B, L, E, H = (4, 64, 256, 32)
        S = E // H
        EXTRA_MAA, EXTRA_DECAY = (32, 64)
        EPS = 1e-05

        def _ln(x, w, b):
            m = jnp.mean(x, axis=-1, keepdims=True)
            v = jnp.mean((x - m) ** 2, axis=-1, keepdims=True)
            return (x - m) * jax.lax.rsqrt(v + EPS) * w + b

        def _token_shift(xn, prev_row):
            first = (prev_row - xn[:, 0])[:, None]
            rest = xn[:, :-1] - xn[:, 1:]
            return jnp.concatenate([first, rest], axis=1)
        key = jax.random.key(seed)
        ks = jax.random.split(key, 24)
        rn = lambda k, shp, s=1.0: jax.random.normal(k, shp, dtype=jnp.float32) * s
        return dict(x=rn(ks[0], (B, L, E)), state=rn(ks[1], (B, 2 + S, E), 0.1), ln1_w=jnp.ones((E,), jnp.float32), ln1_b=jnp.zeros((E,), jnp.float32), ln2_w=jnp.ones((E,), jnp.float32), ln2_b=jnp.zeros((E,), jnp.float32), maa_x=rn(ks[2], (E,), 0.02), maa_w1=rn(ks[3], (E, 5 * EXTRA_MAA), 0.02), maa_w2=rn(ks[4], (5, EXTRA_MAA, E), 0.02), maa_stack=rn(ks[5], (5, E), 0.02), time_decay=rn(ks[6], (E,), 0.5), decay_w1=rn(ks[7], (E, EXTRA_DECAY), 0.02), decay_w2=rn(ks[8], (EXTRA_DECAY, E), 0.02), faaaa=rn(ks[9], (H, S), 0.1), Wr=rn(ks[10], (E, E), 0.02), Wk=rn(ks[11], (E, E), 0.02), Wv=rn(ks[12], (E, E), 0.02), Wg=rn(ks[13], (E, E), 0.02), Wo=rn(ks[14], (E, E), 0.02), gn_w=jnp.ones((E,), jnp.float32), gn_b=jnp.zeros((E,), jnp.float32), ffn_maa_k=rn(ks[15], (E,), 0.02), ffn_maa_r=rn(ks[16], (E,), 0.02), ffn_Wk=rn(ks[17], (E, E), 0.02), ffn_Wr=rn(ks[18], (E, E), 0.02), ffn_Wv=rn(ks[19], (E, E), 0.02), i=0)
    _L0_xattn_all = _L0_xattn_setup()
    _L0_xattn_in = {k: v for k, v in _L0_xattn_all.items() if k in ('ln1_w', 'ln1_b', 'ln2_w', 'ln2_b', 'maa_x', 'maa_w1', 'maa_w2', 'maa_stack', 'time_decay', 'decay_w1', 'decay_w2', 'faaaa', 'Wr', 'Wk', 'Wv', 'Wg', 'Wo', 'gn_w', 'gn_b', 'ffn_maa_k', 'ffn_maa_r', 'ffn_Wk', 'ffn_Wr', 'ffn_Wv')}
    del _L0_xattn_all

    def _L1_xattn_setup():
        import jax, jax.numpy as jnp
        import numpy as np
        HIDDEN = 256
        HEADS = 16
        HEAD_DIM = HIDDEN // HEADS
        LN_EPS = 1e-05
        GATE_INIT = 0.5

        def _layer_norm(x, gamma, beta):
            mu = jnp.mean(x, axis=-1, keepdims=True)
            var = jnp.mean(jnp.square(x - mu), axis=-1, keepdims=True)
            return (x - mu) * jax.lax.rsqrt(var + LN_EPS) * gamma + beta
        key = jax.random.key(seed)
        ks = jax.random.split(key, 8)
        B, T_TEXT, T_AUDIO = (4, 256, 1500)
        s = 0.02
        return {'hidden_states': jax.random.normal(ks[0], (B, T_TEXT, HIDDEN), jnp.float32), 'audio_kv': jax.random.normal(ks[1], (B, T_AUDIO, HIDDEN), jnp.float32), 'audio_attention_mask': jnp.ones((B, T_AUDIO), dtype=bool), 'Wq': jax.random.normal(ks[2], (HIDDEN, HIDDEN), jnp.float32) * s, 'Wk': jax.random.normal(ks[3], (HIDDEN, HIDDEN), jnp.float32) * s, 'Wv': jax.random.normal(ks[4], (HIDDEN, HIDDEN), jnp.float32) * s, 'Wo': jax.random.normal(ks[5], (HIDDEN, HIDDEN), jnp.float32) * s, 'ln_gamma': jnp.ones((HIDDEN,), jnp.float32), 'ln_beta': jnp.zeros((HIDDEN,), jnp.float32), 'gate': jnp.array([GATE_INIT], jnp.float32)}
    _L1_xattn_all = _L1_xattn_setup()
    _L1_xattn_in = {k: v for k, v in _L1_xattn_all.items() if k in ('Wq', 'Wk', 'Wv', 'Wo', 'ln_gamma', 'ln_beta', 'gate')}
    del _L1_xattn_all

    def _L2_xattn_setup():
        import jax, jax.numpy as jnp
        import numpy as np
        N_HEAD = 32
        EPS = 1e-05

        def _ln(x, w, b):
            m = jnp.mean(x, axis=-1, keepdims=True)
            v = jnp.mean((x - m) ** 2, axis=-1, keepdims=True)
            return (x - m) * jax.lax.rsqrt(v + EPS) * w + b

        def _forward(x, state, i, ln1_w, ln1_b, ln2_w, ln2_b, maa_x, maa_w, maa_k, maa_v, maa_r, maa_g, maa_w1, maa_w2, time_decay, decay_w1, decay_w2, faaaa, Wr, Wk, Wv, Wg, Wo, gn_w, gn_b, fmaa_k, fmaa_r, fWk, fWr, fWv):
            B, L, C = x.shape
            H = N_HEAD
            S = C // H
            i0 = (2 + S) * i
            xa = _ln(x, ln1_w, ln1_b)
            sx = jnp.concatenate([state[:, i0 + 1][:, None], xa[:, :-1]], axis=1) - xa
            xxx = xa + sx * maa_x
            t = jnp.tanh(xxx @ maa_w1).reshape(B, L, 5, -1)
            m = jnp.einsum('blfd,fdc->blfc', t, maa_w2)
            mw, mk, mv, mr, mg = (m[:, :, j] for j in range(5))
            xw = xa + sx * (maa_w + mw)
            xk = xa + sx * (maa_k + mk)
            xv = xa + sx * (maa_v + mv)
            xr = xa + sx * (maa_r + mr)
            xg = xa + sx * (maa_g + mg)
            w = time_decay + jnp.tanh(xw @ decay_w1) @ decay_w2
            w = jnp.exp(-jnp.exp(w)).reshape(B, L, H, S)
            r = (xr @ Wr.T).reshape(B, L, H, S)
            k = (xk @ Wk.T).reshape(B, L, H, S)
            v = (xv @ Wv.T).reshape(B, L, H, S)
            g = jax.nn.silu(xg @ Wg.T)
            s0 = state[:, i0 + 2:i0 + 2 + S].reshape(B, H, S, S)

            def step(s, inp):
                k_l, v_l, w_l, r_l = inp
                a = k_l[..., :, None] * v_l[..., None, :]
                out = jnp.einsum('bhs,bhst->bht', r_l, faaaa * a + s)
                s_new = a + w_l[..., None] * s
                return (s_new, out)
            seq = tuple((z.transpose(1, 0, 2, 3) for z in (k, v, w, r)))
            _, outs = jax.lax.scan(step, s0, seq)
            y = outs.transpose(1, 0, 2, 3)
            gm = jnp.mean(y, axis=-1, keepdims=True)
            gv = jnp.mean((y - gm) ** 2, axis=-1, keepdims=True)
            y = ((y - gm) * jax.lax.rsqrt(gv + EPS)).reshape(B, L, C) * gn_w + gn_b
            x = x + y * g @ Wo.T
            xc = _ln(x, ln2_w, ln2_b)
            sxc = jnp.concatenate([state[:, i0][:, None], xc[:, :-1]], axis=1) - xc
            xk2 = xc + sxc * fmaa_k
            xr2 = xc + sxc * fmaa_r
            rr = jax.nn.sigmoid(xr2 @ fWr.T)
            kk = jnp.square(jax.nn.relu(xk2 @ fWk.T))
            x = x + rr * (kk @ fWv.T)
            return x
        key = jax.random.key(seed)
        B, L, C, H = (8, 64, 256, N_HEAD)
        S = C // H
        DM, DD = (32, 64)
        ks = jax.random.split(key, 32)
        n = lambda k, shp, s=1.0: jax.random.normal(k, shp, dtype=jnp.float32) * s
        u = lambda k, shp: jax.random.uniform(k, shp, dtype=jnp.float32)
        inp = {'x': n(ks[0], (B, L, C)), 'state': n(ks[1], (B, 2 + S, C), 0.1), 'i': 0, 'ln1_w': jnp.ones((C,), jnp.float32), 'ln1_b': jnp.zeros((C,), jnp.float32), 'ln2_w': jnp.ones((C,), jnp.float32), 'ln2_b': jnp.zeros((C,), jnp.float32), 'maa_x': u(ks[2], (C,)), 'maa_w': u(ks[3], (C,)), 'maa_k': u(ks[4], (C,)), 'maa_v': u(ks[5], (C,)), 'maa_r': u(ks[6], (C,)), 'maa_g': u(ks[7], (C,)), 'maa_w1': n(ks[8], (C, 5 * DM), 0.02), 'maa_w2': n(ks[9], (5, DM, C), 0.02), 'time_decay': n(ks[10], (C,), 0.5), 'decay_w1': n(ks[11], (C, DD), 0.02), 'decay_w2': n(ks[12], (DD, C), 0.02), 'faaaa': n(ks[13], (H, S, 1), 0.1), 'Wr': n(ks[14], (C, C), 0.02), 'Wk': n(ks[15], (C, C), 0.02), 'Wv': n(ks[16], (C, C), 0.02), 'Wg': n(ks[17], (C, C), 0.02), 'Wo': n(ks[18], (C, C), 0.02), 'gn_w': jnp.ones((C,), jnp.float32), 'gn_b': jnp.zeros((C,), jnp.float32), 'fmaa_k': u(ks[19], (C,)), 'fmaa_r': u(ks[20], (C,)), 'fWk': n(ks[21], (C, C), 0.02), 'fWr': n(ks[22], (C, C), 0.02), 'fWv': n(ks[23], (C, C), 0.02)}
        return inp
    _L2_xattn_all = _L2_xattn_setup()
    _L2_xattn_in = {k: v for k, v in _L2_xattn_all.items() if k in ('ln1_w', 'ln1_b', 'ln2_w', 'ln2_b', 'maa_x', 'maa_w', 'maa_k', 'maa_v', 'maa_r', 'maa_g', 'maa_w1', 'maa_w2', 'time_decay', 'decay_w1', 'decay_w2', 'faaaa', 'Wr', 'Wk', 'Wv', 'Wg', 'Wo', 'gn_w', 'gn_b', 'fmaa_k', 'fmaa_r', 'fWk', 'fWr', 'fWv')}
    del _L2_xattn_all

    def _L3_xattn_setup():
        import jax, jax.numpy as jnp
        import numpy as np
        D = 256
        H = 16
        HD = D // H
        INNER = 4 * D
        EPS = 1e-05

        def layer_norm(x, w, b):
            mu = jnp.mean(x, axis=-1, keepdims=True)
            var = jnp.mean(jnp.square(x - mu), axis=-1, keepdims=True)
            return (x - mu) * jax.lax.rsqrt(var + EPS) * w + b
        key = jax.random.key(seed)
        ks = jax.random.split(key, 12)
        B, LQ, LK = (4, 128, 256)
        std = 0.02
        inp = {'hidden_states': jax.random.normal(ks[0], (B, LQ, D), jnp.float32), 'encoder_hidden_states': jax.random.normal(ks[1], (B, LK, D), jnp.float32), 'encoder_attention_mask': jnp.ones((B, LK), dtype=bool), 'ln1_w': jnp.ones((D,), jnp.float32), 'ln1_b': jnp.zeros((D,), jnp.float32), 'q_w': jax.random.normal(ks[2], (D, D), jnp.float32) * std, 'q_b': jnp.zeros((D,), jnp.float32), 'k_w': jax.random.normal(ks[3], (D, D), jnp.float32) * std, 'k_b': jnp.zeros((D,), jnp.float32), 'v_w': jax.random.normal(ks[4], (D, D), jnp.float32) * std, 'v_b': jnp.zeros((D,), jnp.float32), 'cproj_w': jax.random.normal(ks[5], (D, D), jnp.float32) * std, 'cproj_b': jnp.zeros((D,), jnp.float32), 'ln2_w': jnp.ones((D,), jnp.float32), 'ln2_b': jnp.zeros((D,), jnp.float32), 'fc_w': jax.random.normal(ks[6], (D, INNER), jnp.float32) * std, 'fc_b': jnp.zeros((INNER,), jnp.float32), 'proj_w': jax.random.normal(ks[7], (INNER, D), jnp.float32) * std, 'proj_b': jnp.zeros((D,), jnp.float32)}
        return inp
    _L3_xattn_all = _L3_xattn_setup()
    _L3_xattn_in = {k: v for k, v in _L3_xattn_all.items() if k in ('ln1_w', 'ln1_b', 'q_w', 'q_b', 'k_w', 'k_b', 'v_w', 'v_b', 'cproj_w', 'cproj_b', 'ln2_w', 'ln2_b', 'fc_w', 'fc_b', 'proj_w', 'proj_b')}
    del _L3_xattn_all
    return {'x': x, 'ctx_2048': ctx_2048, 'mask_BxS2_bf1': mask_BxS2_bf1, 'L0_xattn_ln1_w': _L0_xattn_in['ln1_w'], 'L0_xattn_ln1_b': _L0_xattn_in['ln1_b'], 'L0_xattn_ln2_w': _L0_xattn_in['ln2_w'], 'L0_xattn_ln2_b': _L0_xattn_in['ln2_b'], 'L0_xattn_maa_x': _L0_xattn_in['maa_x'], 'L0_xattn_maa_w1': _L0_xattn_in['maa_w1'], 'L0_xattn_maa_w2': _L0_xattn_in['maa_w2'], 'L0_xattn_maa_stack': _L0_xattn_in['maa_stack'], 'L0_xattn_time_decay': _L0_xattn_in['time_decay'], 'L0_xattn_decay_w1': _L0_xattn_in['decay_w1'], 'L0_xattn_decay_w2': _L0_xattn_in['decay_w2'], 'L0_xattn_faaaa': _L0_xattn_in['faaaa'], 'L0_xattn_Wr': _L0_xattn_in['Wr'], 'L0_xattn_Wk': _L0_xattn_in['Wk'], 'L0_xattn_Wv': _L0_xattn_in['Wv'], 'L0_xattn_Wg': _L0_xattn_in['Wg'], 'L0_xattn_Wo': _L0_xattn_in['Wo'], 'L0_xattn_gn_w': _L0_xattn_in['gn_w'], 'L0_xattn_gn_b': _L0_xattn_in['gn_b'], 'L0_xattn_ffn_maa_k': _L0_xattn_in['ffn_maa_k'], 'L0_xattn_ffn_maa_r': _L0_xattn_in['ffn_maa_r'], 'L0_xattn_ffn_Wk': _L0_xattn_in['ffn_Wk'], 'L0_xattn_ffn_Wr': _L0_xattn_in['ffn_Wr'], 'L0_xattn_ffn_Wv': _L0_xattn_in['ffn_Wv'], 'L1_xattn_Wq': _L1_xattn_in['Wq'], 'L1_xattn_Wk': _L1_xattn_in['Wk'], 'L1_xattn_Wv': _L1_xattn_in['Wv'], 'L1_xattn_Wo': _L1_xattn_in['Wo'], 'L1_xattn_ln_gamma': _L1_xattn_in['ln_gamma'], 'L1_xattn_ln_beta': _L1_xattn_in['ln_beta'], 'L1_xattn_gate': _L1_xattn_in['gate'], 'L2_xattn_ln1_w': _L2_xattn_in['ln1_w'], 'L2_xattn_ln1_b': _L2_xattn_in['ln1_b'], 'L2_xattn_ln2_w': _L2_xattn_in['ln2_w'], 'L2_xattn_ln2_b': _L2_xattn_in['ln2_b'], 'L2_xattn_maa_x': _L2_xattn_in['maa_x'], 'L2_xattn_maa_w': _L2_xattn_in['maa_w'], 'L2_xattn_maa_k': _L2_xattn_in['maa_k'], 'L2_xattn_maa_v': _L2_xattn_in['maa_v'], 'L2_xattn_maa_r': _L2_xattn_in['maa_r'], 'L2_xattn_maa_g': _L2_xattn_in['maa_g'], 'L2_xattn_maa_w1': _L2_xattn_in['maa_w1'], 'L2_xattn_maa_w2': _L2_xattn_in['maa_w2'], 'L2_xattn_time_decay': _L2_xattn_in['time_decay'], 'L2_xattn_decay_w1': _L2_xattn_in['decay_w1'], 'L2_xattn_decay_w2': _L2_xattn_in['decay_w2'], 'L2_xattn_faaaa': _L2_xattn_in['faaaa'], 'L2_xattn_Wr': _L2_xattn_in['Wr'], 'L2_xattn_Wk': _L2_xattn_in['Wk'], 'L2_xattn_Wv': _L2_xattn_in['Wv'], 'L2_xattn_Wg': _L2_xattn_in['Wg'], 'L2_xattn_Wo': _L2_xattn_in['Wo'], 'L2_xattn_gn_w': _L2_xattn_in['gn_w'], 'L2_xattn_gn_b': _L2_xattn_in['gn_b'], 'L2_xattn_fmaa_k': _L2_xattn_in['fmaa_k'], 'L2_xattn_fmaa_r': _L2_xattn_in['fmaa_r'], 'L2_xattn_fWk': _L2_xattn_in['fWk'], 'L2_xattn_fWr': _L2_xattn_in['fWr'], 'L2_xattn_fWv': _L2_xattn_in['fWv'], 'L3_xattn_ln1_w': _L3_xattn_in['ln1_w'], 'L3_xattn_ln1_b': _L3_xattn_in['ln1_b'], 'L3_xattn_q_w': _L3_xattn_in['q_w'], 'L3_xattn_q_b': _L3_xattn_in['q_b'], 'L3_xattn_k_w': _L3_xattn_in['k_w'], 'L3_xattn_k_b': _L3_xattn_in['k_b'], 'L3_xattn_v_w': _L3_xattn_in['v_w'], 'L3_xattn_v_b': _L3_xattn_in['v_b'], 'L3_xattn_cproj_w': _L3_xattn_in['cproj_w'], 'L3_xattn_cproj_b': _L3_xattn_in['cproj_b'], 'L3_xattn_ln2_w': _L3_xattn_in['ln2_w'], 'L3_xattn_ln2_b': _L3_xattn_in['ln2_b'], 'L3_xattn_fc_w': _L3_xattn_in['fc_w'], 'L3_xattn_fc_b': _L3_xattn_in['fc_b'], 'L3_xattn_proj_w': _L3_xattn_in['proj_w'], 'L3_xattn_proj_b': _L3_xattn_in['proj_b']}

def reference(x, ctx_2048, mask_BxS2_bf1, L0_xattn_ln1_w, L0_xattn_ln1_b, L0_xattn_ln2_w, L0_xattn_ln2_b, L0_xattn_maa_x, L0_xattn_maa_w1, L0_xattn_maa_w2, L0_xattn_maa_stack, L0_xattn_time_decay, L0_xattn_decay_w1, L0_xattn_decay_w2, L0_xattn_faaaa, L0_xattn_Wr, L0_xattn_Wk, L0_xattn_Wv, L0_xattn_Wg, L0_xattn_Wo, L0_xattn_gn_w, L0_xattn_gn_b, L0_xattn_ffn_maa_k, L0_xattn_ffn_maa_r, L0_xattn_ffn_Wk, L0_xattn_ffn_Wr, L0_xattn_ffn_Wv, L1_xattn_Wq, L1_xattn_Wk, L1_xattn_Wv, L1_xattn_Wo, L1_xattn_ln_gamma, L1_xattn_ln_beta, L1_xattn_gate, L2_xattn_ln1_w, L2_xattn_ln1_b, L2_xattn_ln2_w, L2_xattn_ln2_b, L2_xattn_maa_x, L2_xattn_maa_w, L2_xattn_maa_k, L2_xattn_maa_v, L2_xattn_maa_r, L2_xattn_maa_g, L2_xattn_maa_w1, L2_xattn_maa_w2, L2_xattn_time_decay, L2_xattn_decay_w1, L2_xattn_decay_w2, L2_xattn_faaaa, L2_xattn_Wr, L2_xattn_Wk, L2_xattn_Wv, L2_xattn_Wg, L2_xattn_Wo, L2_xattn_gn_w, L2_xattn_gn_b, L2_xattn_fmaa_k, L2_xattn_fmaa_r, L2_xattn_fWk, L2_xattn_fWr, L2_xattn_fWv, L3_xattn_ln1_w, L3_xattn_ln1_b, L3_xattn_q_w, L3_xattn_q_b, L3_xattn_k_w, L3_xattn_k_b, L3_xattn_v_w, L3_xattn_v_b, L3_xattn_cproj_w, L3_xattn_cproj_b, L3_xattn_ln2_w, L3_xattn_ln2_b, L3_xattn_fc_w, L3_xattn_fc_b, L3_xattn_proj_w, L3_xattn_proj_b):
    import jax
    import jax.numpy as jnp

    def _L0_xattn_ref(x, state, ln1_w, ln1_b, ln2_w, ln2_b, maa_x, maa_w1, maa_w2, maa_stack, time_decay, decay_w1, decay_w2, faaaa, Wr, Wk, Wv, Wg, Wo, gn_w, gn_b, ffn_maa_k, ffn_maa_r, ffn_Wk, ffn_Wr, ffn_Wv, i):
        import jax, jax.numpy as jnp
        import numpy as np
        B, L, E, H = (4, 64, 256, 32)
        S = E // H
        EXTRA_MAA, EXTRA_DECAY = (32, 64)
        EPS = 1e-05

        def _ln(x, w, b):
            m = jnp.mean(x, axis=-1, keepdims=True)
            v = jnp.mean((x - m) ** 2, axis=-1, keepdims=True)
            return (x - m) * jax.lax.rsqrt(v + EPS) * w + b

        def _token_shift(xn, prev_row):
            first = (prev_row - xn[:, 0])[:, None]
            rest = xn[:, :-1] - xn[:, 1:]
            return jnp.concatenate([first, rest], axis=1)
        b, l = (x.shape[0], x.shape[1])
        i0 = (2 + S) * i + 0
        i1 = (2 + S) * i + 1
        xn = _ln(x, ln1_w, ln1_b)
        sx = _token_shift(xn, state[:, i1])
        xxx = jnp.tanh((xn + sx * maa_x) @ maa_w1).reshape(b, l, 5, 1, EXTRA_MAA)
        xxx = jnp.matmul(xxx, maa_w2).reshape(b, l, 5, E)
        x5 = xn[:, :, None] + sx[:, :, None] * (maa_stack + xxx)
        w = jnp.exp(-jnp.exp(time_decay + jnp.tanh(x5[:, :, 1] @ decay_w1) @ decay_w2))
        w = w.reshape(b, l, H, S)
        r = (x5[:, :, 3] @ Wr.T).reshape(b, l, H, S)
        k = (x5[:, :, 0] @ Wk.T).reshape(b, l, H, S)
        v = (x5[:, :, 2] @ Wv.T).reshape(b, l, H, S)
        g = jax.nn.silu(x5[:, :, 4] @ Wg.T)
        s0 = state[:, (2 + S) * i + 2:(2 + S) * (i + 1)].reshape(b, H, S, S)
        u = faaaa[None, :, :, None]

        def step(s, rkvw):
            r_t, k_t, v_t, w_t = rkvw
            a = k_t[:, :, :, None] * v_t[:, :, None, :]
            out = jnp.einsum('bhk,bhkd->bhd', r_t, u * a + s)
            return (a + w_t[:, :, :, None] * s, out)
        xs = tuple((jnp.moveaxis(t, 1, 0) for t in (r, k, v, w)))
        _, outs = jax.lax.scan(step, s0, xs)
        att = jnp.moveaxis(outs, 0, 1).reshape(b, l, E)
        a4 = att.reshape(b, l, H, S)
        m = jnp.mean(a4, axis=-1, keepdims=True)
        var = jnp.mean((a4 - m) ** 2, axis=-1, keepdims=True)
        att = ((a4 - m) * jax.lax.rsqrt(var + EPS)).reshape(b, l, E) * gn_w + gn_b
        x = x + att * g @ Wo.T
        xn2 = _ln(x, ln2_w, ln2_b)
        sx2 = _token_shift(xn2, state[:, i0])
        xk = xn2 + sx2 * ffn_maa_k
        xr = xn2 + sx2 * ffn_maa_r
        rr = jax.nn.sigmoid(xr @ ffn_Wr.T)
        kk = jnp.square(jax.nn.relu(xk @ ffn_Wk.T))
        x = x + rr * (kk @ ffn_Wv.T)
        return x

    def _L1_xattn_ref(hidden_states, audio_kv, audio_attention_mask, Wq, Wk, Wv, Wo, ln_gamma, ln_beta, gate):
        import jax, jax.numpy as jnp
        import numpy as np
        HIDDEN = 256
        HEADS = 16
        HEAD_DIM = HIDDEN // HEADS
        LN_EPS = 1e-05
        GATE_INIT = 0.5

        def _layer_norm(x, gamma, beta):
            mu = jnp.mean(x, axis=-1, keepdims=True)
            var = jnp.mean(jnp.square(x - mu), axis=-1, keepdims=True)
            return (x - mu) * jax.lax.rsqrt(var + LN_EPS) * gamma + beta
        B, Tt, D = hidden_states.shape
        Ta = audio_kv.shape[1]
        scale = HEAD_DIM ** (-0.5)
        a = _layer_norm(audio_kv, ln_gamma, ln_beta)
        Q = (hidden_states @ Wq.T).reshape(B, Tt, HEADS, HEAD_DIM).transpose(0, 2, 1, 3)
        K = (a @ Wk.T).reshape(B, Ta, HEADS, HEAD_DIM).transpose(0, 2, 1, 3)
        V = (a @ Wv.T).reshape(B, Ta, HEADS, HEAD_DIM).transpose(0, 2, 1, 3)
        scores = jnp.einsum('bhtd,bhsd->bhts', Q, K) * scale
        mask = audio_attention_mask[:, None, None, :]
        scores = jnp.where(mask, scores, jnp.float32(-jnp.inf))
        attn = jax.nn.softmax(scores, axis=-1)
        out = jnp.einsum('bhts,bhsd->bhtd', attn, V)
        out = out.transpose(0, 2, 1, 3).reshape(B, Tt, D)
        out = out @ Wo.T
        return hidden_states + jnp.tanh(gate) * out

    def _L2_xattn_ref(x, state, i, ln1_w, ln1_b, ln2_w, ln2_b, maa_x, maa_w, maa_k, maa_v, maa_r, maa_g, maa_w1, maa_w2, time_decay, decay_w1, decay_w2, faaaa, Wr, Wk, Wv, Wg, Wo, gn_w, gn_b, fmaa_k, fmaa_r, fWk, fWr, fWv):
        import jax, jax.numpy as jnp
        import numpy as np
        N_HEAD = 32
        EPS = 1e-05

        def _ln(x, w, b):
            m = jnp.mean(x, axis=-1, keepdims=True)
            v = jnp.mean((x - m) ** 2, axis=-1, keepdims=True)
            return (x - m) * jax.lax.rsqrt(v + EPS) * w + b

        def _forward(x, state, i, ln1_w, ln1_b, ln2_w, ln2_b, maa_x, maa_w, maa_k, maa_v, maa_r, maa_g, maa_w1, maa_w2, time_decay, decay_w1, decay_w2, faaaa, Wr, Wk, Wv, Wg, Wo, gn_w, gn_b, fmaa_k, fmaa_r, fWk, fWr, fWv):
            B, L, C = x.shape
            H = N_HEAD
            S = C // H
            i0 = (2 + S) * i
            xa = _ln(x, ln1_w, ln1_b)
            sx = jnp.concatenate([state[:, i0 + 1][:, None], xa[:, :-1]], axis=1) - xa
            xxx = xa + sx * maa_x
            t = jnp.tanh(xxx @ maa_w1).reshape(B, L, 5, -1)
            m = jnp.einsum('blfd,fdc->blfc', t, maa_w2)
            mw, mk, mv, mr, mg = (m[:, :, j] for j in range(5))
            xw = xa + sx * (maa_w + mw)
            xk = xa + sx * (maa_k + mk)
            xv = xa + sx * (maa_v + mv)
            xr = xa + sx * (maa_r + mr)
            xg = xa + sx * (maa_g + mg)
            w = time_decay + jnp.tanh(xw @ decay_w1) @ decay_w2
            w = jnp.exp(-jnp.exp(w)).reshape(B, L, H, S)
            r = (xr @ Wr.T).reshape(B, L, H, S)
            k = (xk @ Wk.T).reshape(B, L, H, S)
            v = (xv @ Wv.T).reshape(B, L, H, S)
            g = jax.nn.silu(xg @ Wg.T)
            s0 = state[:, i0 + 2:i0 + 2 + S].reshape(B, H, S, S)

            def step(s, inp):
                k_l, v_l, w_l, r_l = inp
                a = k_l[..., :, None] * v_l[..., None, :]
                out = jnp.einsum('bhs,bhst->bht', r_l, faaaa * a + s)
                s_new = a + w_l[..., None] * s
                return (s_new, out)
            seq = tuple((z.transpose(1, 0, 2, 3) for z in (k, v, w, r)))
            _, outs = jax.lax.scan(step, s0, seq)
            y = outs.transpose(1, 0, 2, 3)
            gm = jnp.mean(y, axis=-1, keepdims=True)
            gv = jnp.mean((y - gm) ** 2, axis=-1, keepdims=True)
            y = ((y - gm) * jax.lax.rsqrt(gv + EPS)).reshape(B, L, C) * gn_w + gn_b
            x = x + y * g @ Wo.T
            xc = _ln(x, ln2_w, ln2_b)
            sxc = jnp.concatenate([state[:, i0][:, None], xc[:, :-1]], axis=1) - xc
            xk2 = xc + sxc * fmaa_k
            xr2 = xc + sxc * fmaa_r
            rr = jax.nn.sigmoid(xr2 @ fWr.T)
            kk = jnp.square(jax.nn.relu(xk2 @ fWk.T))
            x = x + rr * (kk @ fWv.T)
            return x
        return _forward(x, state, i, ln1_w, ln1_b, ln2_w, ln2_b, maa_x, maa_w, maa_k, maa_v, maa_r, maa_g, maa_w1, maa_w2, time_decay, decay_w1, decay_w2, faaaa, Wr, Wk, Wv, Wg, Wo, gn_w, gn_b, fmaa_k, fmaa_r, fWk, fWr, fWv)

    def _L3_xattn_ref(hidden_states, encoder_hidden_states, encoder_attention_mask, ln1_w, ln1_b, q_w, q_b, k_w, k_b, v_w, v_b, cproj_w, cproj_b, ln2_w, ln2_b, fc_w, fc_b, proj_w, proj_b):
        import jax, jax.numpy as jnp
        import numpy as np
        D = 256
        H = 16
        HD = D // H
        INNER = 4 * D
        EPS = 1e-05

        def layer_norm(x, w, b):
            mu = jnp.mean(x, axis=-1, keepdims=True)
            var = jnp.mean(jnp.square(x - mu), axis=-1, keepdims=True)
            return (x - mu) * jax.lax.rsqrt(var + EPS) * w + b
        B, LQ, _ = hidden_states.shape
        LK = encoder_hidden_states.shape[1]
        residual = hidden_states
        x = layer_norm(hidden_states, ln1_w, ln1_b)
        q = (x @ q_w + q_b).reshape(B, LQ, H, HD).transpose(0, 2, 1, 3)
        k = (encoder_hidden_states @ k_w + k_b).reshape(B, LK, H, HD).transpose(0, 2, 1, 3)
        v = (encoder_hidden_states @ v_w + v_b).reshape(B, LK, H, HD).transpose(0, 2, 1, 3)
        scale = 1.0 / np.sqrt(HD).astype(np.float32)
        scores = jnp.einsum('bhqd,bhkd->bhqk', q, k) * scale
        mask = encoder_attention_mask[:, None, None, :]
        mask_value = jnp.finfo(scores.dtype).min
        scores = jnp.where(mask, scores, mask_value)
        attn = jax.nn.softmax(scores, axis=-1)
        out = jnp.einsum('bhqk,bhkd->bhqd', attn, v)
        out = out.transpose(0, 2, 1, 3).reshape(B, LQ, D)
        out = out @ cproj_w + cproj_b
        hidden = out + residual
        residual = hidden
        y = layer_norm(hidden, ln2_w, ln2_b)
        y = jax.nn.gelu(y @ fc_w + fc_b, approximate=True)
        y = y @ proj_w + proj_b
        return residual + y
    x = _L0_xattn_ref(x, ctx_2048, L0_xattn_ln1_w, L0_xattn_ln1_b, L0_xattn_ln2_w, L0_xattn_ln2_b, L0_xattn_maa_x, L0_xattn_maa_w1, L0_xattn_maa_w2, L0_xattn_maa_stack, L0_xattn_time_decay, L0_xattn_decay_w1, L0_xattn_decay_w2, L0_xattn_faaaa, L0_xattn_Wr, L0_xattn_Wk, L0_xattn_Wv, L0_xattn_Wg, L0_xattn_Wo, L0_xattn_gn_w, L0_xattn_gn_b, L0_xattn_ffn_maa_k, L0_xattn_ffn_maa_r, L0_xattn_ffn_Wk, L0_xattn_ffn_Wr, L0_xattn_ffn_Wv, 0)
    x = _L1_xattn_ref(x, ctx_2048, mask_BxS2_bf1, L1_xattn_Wq, L1_xattn_Wk, L1_xattn_Wv, L1_xattn_Wo, L1_xattn_ln_gamma, L1_xattn_ln_beta, L1_xattn_gate)
    x = _L2_xattn_ref(x, ctx_2048, 0, L2_xattn_ln1_w, L2_xattn_ln1_b, L2_xattn_ln2_w, L2_xattn_ln2_b, L2_xattn_maa_x, L2_xattn_maa_w, L2_xattn_maa_k, L2_xattn_maa_v, L2_xattn_maa_r, L2_xattn_maa_g, L2_xattn_maa_w1, L2_xattn_maa_w2, L2_xattn_time_decay, L2_xattn_decay_w1, L2_xattn_decay_w2, L2_xattn_faaaa, L2_xattn_Wr, L2_xattn_Wk, L2_xattn_Wv, L2_xattn_Wg, L2_xattn_Wo, L2_xattn_gn_w, L2_xattn_gn_b, L2_xattn_fmaa_k, L2_xattn_fmaa_r, L2_xattn_fWk, L2_xattn_fWr, L2_xattn_fWv)
    x = _L3_xattn_ref(x, ctx_2048, mask_BxS2_bf1, L3_xattn_ln1_w, L3_xattn_ln1_b, L3_xattn_q_w, L3_xattn_q_b, L3_xattn_k_w, L3_xattn_k_b, L3_xattn_v_w, L3_xattn_v_b, L3_xattn_cproj_w, L3_xattn_cproj_b, L3_xattn_ln2_w, L3_xattn_ln2_b, L3_xattn_fc_w, L3_xattn_fc_b, L3_xattn_proj_w, L3_xattn_proj_b)
    return x

_drawn_inputs = setup_inputs


def setup_inputs(seed=0):
    import zlib

    import numpy as np

    out = dict(_drawn_inputs(seed))
    spreads = {'L0_xattn_ln1_w': (1.0, 0.562),
     'L0_xattn_ln1_b': (0.0, 0.565),
     'L0_xattn_ln2_w': (1.0, 0.6),
     'L0_xattn_ln2_b': (0.0, 0.8),
     'L0_xattn_gn_w': (1.0, 0.6),
     'L0_xattn_gn_b': (0.0, 0.8),
     'L1_xattn_ln_gamma': (1.0, 0.6),
     'L1_xattn_ln_beta': (0.0, 2.0),
     'L2_xattn_ln1_w': (1.0, 0.6),
     'L2_xattn_ln1_b': (0.0, 0.575),
     'L2_xattn_ln2_w': (1.0, 0.6),
     'L2_xattn_ln2_b': (0.0, 0.8),
     'L2_xattn_gn_w': (1.0, 0.6),
     'L2_xattn_gn_b': (0.0, 0.8),
     'L3_xattn_ln1_w': (1.0, 0.6),
     'L3_xattn_ln1_b': (0.0, 2.0),
     'L3_xattn_q_b': (0.0, 2.0),
     'L3_xattn_k_b': (0.0, 2.0),
     'L3_xattn_v_b': (0.0, 2.0),
     'L3_xattn_cproj_b': (0.0, 2.0),
     'L3_xattn_ln2_w': (1.0, 0.6),
     'L3_xattn_ln2_b': (0.0, 2.0),
     'L3_xattn_fc_b': (0.0, 2.0),
     'L3_xattn_proj_b': (0.0, 2.0)}
    factors = {'L0_xattn_maa_x': 8.0,
     'L0_xattn_maa_w1': 6.924,
     'L0_xattn_maa_w2': 6.946,
     'L0_xattn_maa_stack': 8.0,
     'L0_xattn_time_decay': 2.772,
     'L0_xattn_decay_w1': 8.0,
     'L0_xattn_decay_w2': 8.0,
     'L0_xattn_faaaa': 5.46,
     'L0_xattn_ffn_maa_k': 8.0,
     'L0_xattn_ffn_maa_r': 8.0,
     'L0_xattn_ffn_Wk': 3.052,
     'L0_xattn_ffn_Wr': 8.0,
     'L0_xattn_ffn_Wv': 2.828,
     'L1_xattn_Wq': 8.0,
     'L1_xattn_Wk': 8.0,
     'L2_xattn_maa_x': 8.0,
     'L2_xattn_maa_w': 8.0,
     'L2_xattn_maa_w1': 8.0,
     'L2_xattn_maa_w2': 8.0,
     'L2_xattn_time_decay': 3.682,
     'L2_xattn_decay_w1': 8.0,
     'L2_xattn_decay_w2': 8.0,
     'L2_xattn_faaaa': 7.148,
     'L2_xattn_fmaa_k': 7.667,
     'L2_xattn_fmaa_r': 8.0,
     'L2_xattn_fWk': 4.424,
     'L2_xattn_fWr': 8.0,
     'L2_xattn_fWv': 4.041,
     'L3_xattn_q_w': 64.0,
     'L3_xattn_k_w': 64.0,
     'L3_xattn_v_w': 64.0,
     'L3_xattn_cproj_w': 8.0,
     'L3_xattn_fc_w': 8.0,
     'L3_xattn_proj_w': 8.0}
    for name, (base, spread) in spreads.items():
        noise = np.random.default_rng([zlib.crc32(name.encode()), seed]).standard_normal(out[name].shape)
        drawn = base * np.exp(spread * noise) if base else spread * noise
        out[name] = jnp.asarray(drawn.astype(out[name].dtype))
    for name, factor in factors.items():
        out[name] = (out[name] * factor).astype(out[name].dtype)
    return out
```

```python
from contextlib import ExitStack

import concourse.bass as bass
from concourse import mybir

F32 = mybir.dt.float32
U8 = mybir.dt.uint8
ALU = mybir.AluOpType
ACT = mybir.ActivationFunctionType
AX = mybir.AxisListType

P = 128
C = 256
HALF = C // P
T = 128
B = 16
NB = 4
G = B // NB
N = NB * T
RH, RS = 32, 8
MIX, DEC = 32, 64
NMIX = 5
AH, AD = 16, 16
HPQ = 4
FF = 1024
FFT = FF // P
TB = T // 32
DC = 2
NCH = RS // DC
EPS = 1e-5
MASKED = 1e30

RWKV_COLS = [("w1", HALF * NMIX * MIX), ("w2a", C), ("w2b", C), ("dw1", HALF * DEC), ("dw2", C),
             ("Wr", HALF * C), ("Wk", HALF * C), ("Wv", HALF * C), ("Wg", HALF * C), ("Wo", HALF * C),
             ("fWr", HALF * C), ("fWk", HALF * C), ("fWv", HALF * C),
             ("ln_w", 2 * HALF), ("ln_b", 2 * HALF), ("maa_x", HALF), ("maa", NMIX * HALF),
             ("gn_w", HALF), ("gn_b", HALF), ("fk", HALF), ("fr", HALF), ("u", RS)]
ATTN_COLS = [("Wq", HALF * HPQ * P), ("Wk", HALF * HPQ * P), ("Wv", HALF * C), ("Wo", HALF * C),
             ("qb", HPQ), ("kb", HPQ), ("ln_w", 2 * HALF), ("ln_b", 2 * HALF), ("gate", 1)]
MLP_COLS = [("fc", HALF * FF), ("proj", FFT * C), ("fc_b", FFT), ("v_b", C), ("o_b", C), ("proj_b", C)]
COMMON_COLS = [("ident", P), ("ones", P), ("maskrow", P)]


def spans(cols):
    at, out = 0, {}
    for name, n in cols:
        out[name] = (at, at + n)
        at += n
    return out, at


COUNTS = {
    "rwkv": dict(r_stats=2, r_rstd=2, r_z=2, r_zT=4, r_xn=4, r_mixed=8, r_used=8, r_lowrank=1, r_maa=5,
                 r_dec=1, r_decay=1, r_turned=4, r_w=1, r_tg=1, r_rk=1, r_ru=1, r_vr=1, r_s0=4, r_rs=4,
                 r_y=4, r_yc=1, r_sq=1, r_var=1, r_ystd=1, r_yt=1, r_yT=2, r_yn=2, r_yg=1, r_o=1,
                 r_kk=1, r_rr=1, r_fv=1, x_done=1),
    "attn": dict(a_stats=1, a_rstd=1, a_z=1, a_xT=2, a_xc=2, a_cT=2, a_cc=2),
    "attn_mlp": dict(a_stats=2, a_rstd=2, a_z=2, a_xT=4, a_xc=4, a_fc=8, a_gelu=8, a_mlp=1),
}
for _kind in ("attn", "attn_mlp"):
    COUNTS[_kind].update(a_qk=8, a_q=4, a_k=4, a_vp=1, a_v=1, a_vones=1, a_s=16, a_max=16, a_exp=16,
                         a_pT=16, a_pc=16, a_pv=16, a_on=4, a_oT=2, a_oc=2, a_o=1, x_done=1)
COUNTS["attn_mlp"]["x_done"] = 2


class Unit:

    def __init__(self, kind, layer, before):
        self.kind, self.layer = kind, layer
        self.base = {}
        for unit in before:
            for name, n in COUNTS[unit.kind].items():
                self.base[name] = self.base.get(name, 0) + n

    def at(self, name, n):
        return self.base.get(name, 0) + n


def build(nc, x, ctx, ctx_t, s0, state, mask_row, mask_col, rwkv_w, attn_w, mlp_w, common, out):
    rw, rw_n = spans(RWKV_COLS)
    aw, aw_n = spans(ATTN_COLS)
    mw, mw_n = spans(MLP_COLS)
    cw, cw_n = spans(COMMON_COLS)

    with ExitStack() as stack:
        def sb(name, shape, dt=F32):
            return stack.enter_context(nc.sbuf_tensor(name, [P] + shape, dt))

        r_pack = [sb(f"rwkv_w{i}", [rw_n]) for i in range(2)]
        a_pack = [sb(f"attn_w{i}", [aw_n]) for i in range(2)]
        m_pack = sb("mlp_w", [mw_n])
        c_pack = sb("common_w", [cw_n])
        tanh_gate = sb("tanh_gate", [1])
        half_pow = sb("half_pow", [P])

        def r_(layer, name):
            return r_pack[layer][:, rw[name][0]:rw[name][1]]

        def rh_(layer, name):
            return r_(layer, name).rearrange("p (h n) -> p h n", h=HALF)

        def a_(layer, name):
            return a_pack[layer][:, aw[name][0]:aw[name][1]]

        def ah_(layer, name):
            return a_(layer, name).rearrange("p (h n) -> p h n", h=HALF)

        def m_(name):
            return m_pack[:, mw[name][0]:mw[name][1]]

        def c_(name):
            return c_pack[:, cw[name][0]:cw[name][1]]

        ident = c_("ident")
        ones_row = c_("ones")[0:1, :]
        maskrow_sel = c_("maskrow")[0:1, :]

        X = sb("X", [NB, C])
        ctx_sb = sb("ctx_sb", [NB * C])
        ctx_tok = ctx_sb[:].rearrange("p (b c) -> p b c", b=NB)
        ctx_chan = ctx_sb[:].rearrange("p (h n) -> p h n", h=HALF)
        s0_sb = sb("s0_sb", [RS, RS])
        st_sb = sb("st_sb", [2, HALF, NB])
        mrow8 = sb("mrow8", [N], U8)
        mrow = sb("mrow", [N])
        mcol8 = sb("mcol8", [NB], U8)
        mcol = sb("mcol", [NB])

        z = sb("z", [NB, C])
        XN = sb("XN", [HALF, NB, T + 1])
        SX = sb("SX", [HALF, NB, T])
        X5 = [sb(f"X5_{i}", [HALF, NB, T]) for i in range(2)]
        TT = sb("TT", [2, N])
        tmp = sb("tmp", [HALF, NB, T])
        thT = sb("thT", [N])
        E_ = sb("E_", [RS, T])
        W_ = sb("W_", [RS, T])
        K_ = sb("K_", [RS, T])
        V_ = sb("V_", [RS, T])
        R_ = sb("R_", [RS, T])
        VR = sb("VR", [RS, T])
        RU = sb("RU", [T])
        A2 = sb("A2", [2, DC, RS, T])
        A_ = [A2[:, i] for i in range(2)]
        S_ = sb("S_", [DC, RS, T])
        Gt = sb("Gt", [HALF, NB, T])
        small = sb("small", [4, T])
        bn = sb("bn", [NB, 6])
        mv = sb("mv", [NB, 2])
        veps = sb("veps", [T])
        rstd = sb("rstd", [T])

        az = sb("az", [NB, C])
        XT = sb("XT", [HALF, N])
        CT = sb("CT", [HALF, N])
        QK = A2[:].rearrange("p a d k t -> p (a d k t)").rearrange("p (a q n) -> p a q n", a=2, q=HPQ)
        Q_, K2 = QK[:, 0], QK[:, 1]
        H_ = QK.rearrange("p a q n -> p (a q) n")
        VA = sb("VA", [NB, AH, AD + 1])
        pp = S_[:].rearrange("p d k t -> p (d k t)").rearrange("p (a b q t) -> p a b q t", a=2, b=2, q=HPQ)
        PR, PT = pp[:, 0], pp[:, 1]
        nmax = sb("nmax", [2, HPQ])
        rden = sb("rden", [AH])
        abn = sb("abn", [NB, 6])
        amv = sb("amv", [NB, 2])
        aveps = sb("aveps", [NB])
        arstd = sb("arstd", [NB])

        PA = stack.enter_context(nc.psum_tensor("PA", [P, 1024], F32))
        PB = stack.enter_context(nc.psum_tensor("PB", [P, 1024], F32))
        QA = stack.enter_context(nc.psum_tensor("QA", [P, 1024], F32))
        QB = stack.enter_context(nc.psum_tensor("QB", [P, 1024], F32))

        def blocks(buf):
            return buf[:].rearrange("p h b t -> p h (b t)").rearrange("p h (a b t) -> p h a b t", a=TB, b=NB)

        def bank(i):
            return (QA if i < 2 else QB)[:, (i % 2) * 512:(i % 2 + 1) * 512]

        names = sorted({n for k in COUNTS.values() for n in k})
        sem = {n: stack.enter_context(nc.semaphore(n)) for n in names}
        extra = ["loaded_w", "setup_done", "ld_x", "ld_ctx", "ld_ctxT", "ld_small", "st_out",
                 "v_chain", "p_chain", "s_chain", "gate_done", "mask_done"]
        for n in extra:
            sem[n] = stack.enter_context(nc.semaphore(n))

        with nc.Block() as block:
            @block.sync
            def _(sp):
                for i in range(2):
                    sp.dma_start(r_pack[i][:], rwkv_w[i]).then_inc(sem["loaded_w"], 16)
                    sp.dma_start(a_pack[i][:], attn_w[i]).then_inc(sem["loaded_w"], 16)
                sp.dma_start(m_pack[:], mlp_w).then_inc(sem["loaded_w"], 16)
                sp.dma_start(c_pack[:], common).then_inc(sem["loaded_w"], 16)
                sp.wait_ge(sem["loaded_w"], 96)

            @block.gpsimd
            def _(pool):
                nc.gpsimd.memset(half_pow[:], -0.5).then_inc(sem["setup_done"], 1)
                pool.wait_ge(sem["setup_done"], 1)
                nc.gpsimd.memset(thT[DEC:DEC + 1, :], 1.0).then_inc(sem["setup_done"], 1)
                pool.wait_ge(sem["setup_done"], 2)
                nc.gpsimd.memset(W_[:, :, 0:1], 0.0)

            @block.scalar
            def _(act):
                act.wait_ge(sem["loaded_w"], 96)
                nc.scalar.activation(tanh_gate[:], a_(0, "gate"), ACT.Tanh)

        with nc.Fori(0, G) as g:
            units = []
            for kind, layer in (("rwkv", 0), ("attn", 0), ("rwkv", 1), ("attn_mlp", 1)):
                units.append(Unit(kind, layer, list(units)))

            with nc.Block() as block:
                @block.sync
                def _(sp):
                    sp.dma_start(X[:], x[g]).then_inc(sem["ld_x"], 16)
                    sp.dma_start(st_sb[:], state[g]).then_inc(sem["ld_small"], 16)
                    sp.dma_start(s0_sb[:], s0[g]).then_inc(sem["ld_small"], 16)
                    sp.dma_start(mrow8[0:1, :], mask_row[g]).then_inc(sem["ld_small"], 16)
                    sp.dma_start(mcol8[:], mask_col[g]).then_inc(sem["ld_small"], 16)
                    sp.dma_start(ctx_tok, ctx[g]).then_inc(sem["ld_ctx"], 16)
                    sp.wait_ge(sem["a_z"], units[1].at("a_z", 1))
                    sp.dma_start(ctx_chan, ctx_t[g]).then_inc(sem["ld_ctxT"], 16)
                    sp.wait_ge(sem["x_done"], units[3].at("x_done", 2))
                    sp.dma_start(out[g], X[:]).then_inc(sem["st_out"], 16)
                    sp.wait_ge(sem["st_out"], 16)

                @block.vector
                def _(dve):
                    v = nc.vector
                    count = [0]

                    def link(ins):
                        count[0] += 1
                        ins.then_inc(sem["v_chain"], 1)
                        dve.wait_ge(sem["v_chain"], count[0])

                    def norm_stats(src, st, mean_var, done):
                        for b in range(NB):
                            last = v.bn_stats(st[:, b, :], src[:, b, :])
                        link(last)
                        for b in range(NB):
                            last = v.bn_aggr(mean_var[:, b, :], st[:, b, :])
                        last.then_inc(done, 1)

                    def norm_apply(dst, src, mean_var, rs, done):
                        for b in range(NB):
                            last = v.tensor_scalar(dst[:, b, :], src[:, b, :], mean_var[:, b, 0:1], rs[:, b:b + 1],
                                                   ALU.subtract, ALU.mult)
                        last.then_inc(done, 1)

                    def shift_in(u, k):
                        norm_stats(X, bn, mv, sem["r_stats"])
                        dve.wait_ge(sem["r_rstd"], u.at("r_rstd", k + 1))
                        v.tensor_copy(XN[:, :, :, 0], st_sb[:, 1 - k])
                        norm_apply(z, X, mv, rstd, sem["r_z"])
                        dve.wait_ge(sem["r_xn"], u.at("r_xn", 2 * k + 2))
                        link(v.tensor_tensor(SX[:], XN[:, :, :, 0:T], XN[:, :, :, 1:T + 1], ALU.subtract))

                    def mix(u, use, vec):
                        if use >= 2:
                            dve.wait_ge(sem["r_used"], u.at("r_used", use - 1))
                        for h in range(HALF):
                            last = v.scalar_tensor_tensor(X5[use % 2][:, h], SX[:, h], vec[:, h:h + 1],
                                                          XN[:, h, :, 1:T + 1], ALU.mult, ALU.add)
                        last.then_inc(sem["r_mixed"], 1)

                    def mix_low_rank(u, f):
                        dve.wait_ge(sem["r_maa"], u.at("r_maa", f + 1))
                        use = f + 1
                        for h in range(HALF):
                            col = rw["maa"][0] + f * HALF + h
                            last = v.scalar_tensor_tensor(tmp[:, h], PA[:, h * 512:(h + 1) * 512].rearrange("p (b t) -> p b t", b=NB),
                                                          r_pack[u.layer][:, col:col + 1], SX[:, h], ALU.add, ALU.mult)
                        link(last)
                        if use >= 2:
                            dve.wait_ge(sem["r_used"], u.at("r_used", use - 1))
                        split = lambda ap: ap.rearrange("p b (a t) -> p a b t", a=TB)
                        for h in range(HALF):
                            last = v.tensor_tensor(blocks(X5[use % 2])[:, h], split(tmp[:, h]), split(XN[:, h, :, 1:T + 1]), ALU.add)
                        last.then_inc(sem["r_mixed"], 1)

                    def turn(u, n, dst):
                        if n == 0:
                            dve.wait_ge(sem["r_decay"], u.at("r_decay", 1))
                        else:
                            dve.wait_ge(sem["r_used"], u.at("r_used", n + 2))
                        v.transpose(dst[:].rearrange("p k (a t) -> p a k t", a=TB),
                                    PB[:].rearrange("p (a k h) -> p a k h", a=TB, h=32))\
                            .then_inc(sem["r_turned"], 1)

                    def outer(u, c):
                        if c >= 2:
                            dve.wait_ge(sem["r_y"], u.at("r_y", c - 1))
                        return v.tensor_tensor(A_[c % 2][:, :, :, 1:T],
                                        K_[:, :, 0:T - 1].unsqueeze(1).broadcast_to([P, DC, RS, T - 1]),
                                        V_[:, DC * c:DC * c + DC, 0:T - 1].unsqueeze(2).broadcast_to([P, DC, RS, T - 1]),
                                        ALU.mult)

                    def rwkv(u):
                        shift_in(u, 0)
                        mix(u, 0, r_(u.layer, "maa_x"))
                        mix_low_rank(u, 0)
                        mix_low_rank(u, 1)
                        turn(u, 0, E_)
                        mix_low_rank(u, 2)
                        turn(u, 1, K_)
                        mix_low_rank(u, 3)
                        turn(u, 2, V_)
                        mix_low_rank(u, 4)
                        turn(u, 3, R_)
                        dve.wait_ge(sem["r_turned"], u.at("r_turned", 3))
                        link(outer(u, 0))
                        dve.wait_ge(sem["r_tg"], u.at("r_tg", 1))
                        link(v.scalar_tensor_tensor(Gt[:].rearrange("p h b t -> p (h b t)"), Gt[:].rearrange("p h b t -> p (h b t)"),
                                                    1.0, PB[:], ALU.add, ALU.mult))
                        for c in range(NCH):
                            if c + 1 < NCH:
                                link(outer(u, c + 1))
                            dve.wait_ge(sem["r_s0"], u.at("r_s0", c + 1))
                            if c == 0:
                                dve.wait_ge(sem["r_w"], u.at("r_w", 1))
                            else:
                                dve.wait_ge(sem["r_rs"], u.at("r_rs", c))
                            for d in range(DC):
                                last = v.tensor_tensor_scan(S_[:, d].rearrange("p k t -> p (k t)"), W_[:].rearrange("p k t -> p (k t)"),
                                                            A_[c % 2][:, d].rearrange("p k t -> p (k t)"), 0.0, ALU.mult, ALU.add)
                            link(last)
                            v.tensor_tensor(A_[c % 2], R_[:].unsqueeze(1).broadcast_to([P, DC, RS, T]), S_[:], ALU.mult)\
                                .then_inc(sem["r_rs"], 1)
                            if c == 0:
                                dve.wait_ge(sem["r_rk"], u.at("r_rk", 1))
                                v.tensor_reduce(RU[:], tmp[:].rearrange("p h b t -> p (h b) t").rearrange("p k t -> p t k"), AX.X, ALU.add)\
                                    .then_inc(sem["r_ru"], 1)
                        y = PA[:].rearrange("p (d t) -> p d t", d=RS)
                        dve.wait_ge(sem["r_y"], u.at("r_y", NCH))
                        link(v.tensor_reduce(small[:, 0], y.rearrange("p d t -> p t d"), AX.X, ALU.add))
                        yc = z[:].rearrange("p b c -> p (b c)").rearrange("p (d t) -> p d t", d=RS)
                        v.scalar_tensor_tensor(yc, small[:, 0].unsqueeze(1).broadcast_to([P, RS, T]), -1.0 / RS, y,
                                               ALU.mult, ALU.add).then_inc(sem["r_yc"], 1)
                        dve.wait_ge(sem["r_sq"], u.at("r_sq", 1))
                        v.tensor_reduce(small[:, 1], tmp[:].rearrange("p h b t -> p (h b) t").rearrange("p k t -> p t k"), AX.X, ALU.add)\
                            .then_inc(sem["r_var"], 1)
                        dve.wait_ge(sem["r_ystd"], u.at("r_ystd", 1))
                        yn = X5[0][:].rearrange("p h b t -> p (h b) t")
                        dve.wait_ge(sem["r_yc"], u.at("r_yc", 1))
                        link(v.tensor_tensor(yn, yc, rstd[:].unsqueeze(1).broadcast_to([P, RS, T]), ALU.mult))
                        v.transpose(X5[1][:].rearrange("p h b t -> p (h b t)").rearrange("p (a d h) -> p a d h", a=TB, d=RS),
                                    yn.rearrange("p d (a t) -> p a d t", a=TB)).then_inc(sem["r_yt"], 1)
                        dve.wait_ge(sem["r_yn"], u.at("r_yn", 2))
                        for h in range(HALF):
                            last = v.tensor_tensor(SX[:, h].rearrange("p b (a t) -> p a b t", a=TB),
                                                   TT[:, h].rearrange("p (a b t) -> p a b t", a=TB, b=NB), blocks(Gt)[:, h], ALU.mult)
                        last.then_inc(sem["r_yg"], 1)
                        dve.wait_ge(sem["r_o"], u.at("r_o", 1))
                        xf = X[:].rearrange("p b c -> p (b c)")
                        link(v.scalar_tensor_tensor(xf, PA[:], 0.5, xf, ALU.mult, ALU.add))
                        shift_in(u, 1)
                        mix(u, 6, r_(u.layer, "fk"))
                        mix(u, 7, r_(u.layer, "fr"))
                        dve.wait_ge(sem["r_rr"], u.at("r_rr", 1))
                        dve.wait_ge(sem["r_fv"], u.at("r_fv", 1))
                        tf = tmp[:].rearrange("p h b t -> p (h b t)")
                        link(v.scalar_tensor_tensor(tf, R_[:].rearrange("p k t -> p (k t)"), 1.0, PB[:], ALU.add, ALU.mult))
                        v.scalar_tensor_tensor(xf, tf, 0.5, xf, ALU.mult, ALU.add).then_inc(sem["x_done"], 1)
                        dve.wait_ge(sem["x_done"], u.at("x_done", 1))

                    def attn(u):
                        mlp = u.kind == "attn_mlp"
                        xf = X[:].rearrange("p b c -> p (b c)")
                        if mlp:
                            norm_stats(X, abn, amv, sem["a_stats"])
                            dve.wait_ge(sem["a_rstd"], u.at("a_rstd", 1))
                            norm_apply(az, X, amv, arstd, sem["a_z"])
                        else:
                            dve.wait_ge(sem["ld_ctx"], 16)
                            norm_stats(ctx_tok, abn, amv, sem["a_stats"])
                            dve.wait_ge(sem["a_rstd"], u.at("a_rstd", 1))
                            norm_apply(az, ctx_tok, amv, arstd, sem["a_z"])
                        for j in range(HPQ):
                            dve.wait_ge(sem["a_qk"], u.at("a_qk", j + 1))
                            v.tensor_scalar(Q_[:, j], bank(j), a_(u.layer, "qb")[:, j:j + 1], AD ** -0.5, ALU.add, ALU.mult)\
                                .then_inc(sem["a_q"], 1)

                        def biggest(n):
                            dve.wait_ge(sem["a_s"], u.at("a_s", n + 1))
                            v.tensor_reduce(nmax[:, n % 2], bank(2 + n % 2).rearrange("p (h s) -> p h s", h=HPQ), AX.X,
                                            ALU.max, negate=True).then_inc(sem["a_max"], 1)

                        def probs_out(n):
                            dve.wait_ge(sem["a_pT"], u.at("a_pT", n + 1))
                            if n >= 2:
                                dve.wait_ge(sem["a_pv"], u.at("a_pv", n - 1))
                            v.tensor_copy(PT[:, n % 2], bank(0).rearrange("p (h t) -> p h t", h=HPQ))\
                                .then_inc(sem["a_pc"], 1)

                        def normalise(b):
                            dve.wait_ge(sem["a_pv"], u.at("a_pv", HPQ * (b + 1)))
                            o = bank(1)[:, 0:AH * (AD + 1)].rearrange("p (h d) -> p h d", h=AH)
                            link(v.reciprocal(rden[:], o[:, :, AD]))
                            v.tensor_tensor(az[:, b].rearrange("p (h d) -> p h d", h=AH), o[:, :, 0:AD],
                                            rden[:].unsqueeze(2).broadcast_to([P, AH, AD]), ALU.mult)\
                                .then_inc(sem["a_on"], 1)

                        jobs = NB * HPQ
                        for n in range(jobs + 2):
                            if n < jobs:
                                biggest(n)
                            if 1 <= n <= jobs:
                                probs_out(n - 1)
                            if n >= 2 and (n - 2) % HPQ == HPQ - 1:
                                normalise((n - 2) // HPQ)
                        dve.wait_ge(sem["a_o"], u.at("a_o", 1))
                        if not mlp:
                            v.scalar_tensor_tensor(xf, QA[:], tanh_gate[:, 0:1], xf, ALU.mult, ALU.add)\
                                .then_inc(sem["x_done"], 1)
                            dve.wait_ge(sem["x_done"], u.at("x_done", 1))
                            return
                        v.tensor_tensor(xf, QA[:], xf, ALU.add).then_inc(sem["x_done"], 1)
                        dve.wait_ge(sem["x_done"], u.at("x_done", 1))
                        norm_stats(X, abn, amv, sem["a_stats"])
                        dve.wait_ge(sem["a_rstd"], u.at("a_rstd", 2))
                        norm_apply(az, X, amv, arstd, sem["a_z"])
                        dve.wait_ge(sem["a_mlp"], u.at("a_mlp", 1))
                        v.tensor_tensor(xf, QA[:], xf, ALU.add).then_inc(sem["x_done"], 1)

                    dve.wait_ge(sem["ld_small"], 64)
                    link(v.tensor_copy(mrow[0:1, :], mrow8[0:1, :]))
                    v.tensor_scalar(mrow[0:1, :], mrow[0:1, :], 1.0, MASKED, ALU.subtract, ALU.mult)
                    v.tensor_copy(mcol[:], mcol8[:]).then_inc(sem["mask_done"], 1)
                    dve.wait_ge(sem["ld_x"], 16)
                    rwkv(units[0])
                    attn(units[1])
                    rwkv(units[2])
                    attn(units[3])

                @block.gpsimd
                def _(pool):
                    q = nc.gpsimd
                    count = [0]

                    def link(ins):
                        count[0] += 1
                        ins.then_inc(sem["p_chain"], 1)
                        pool.wait_ge(sem["p_chain"], count[0])

                    def inv_std(dst, scratch, var, scale, width, done):
                        link(q.tensor_scalar(scratch, var, scale, EPS, ALU.mult, ALU.add))
                        q.tensor_tensor(dst, scratch, half_pow[:, 0:width], ALU.pow).then_inc(done, 1)

                    def rwkv(u):
                        pool.wait_ge(sem["r_stats"], u.at("r_stats", 1))
                        inv_std(rstd[:, 0:NB], veps[:, 0:NB], mv[:, :, 1], 1.0, NB, sem["r_rstd"])
                        pool.wait_ge(sem["r_turned"], u.at("r_turned", 4))
                        rk = tmp[:].rearrange("p h b t -> p (h b) t")
                        link(q.tensor_tensor(rk, R_[:], K_[:], ALU.mult))
                        q.tensor_tensor(rk, rk, r_(u.layer, "u").unsqueeze(2).broadcast_to([P, RS, T]), ALU.mult)\
                            .then_inc(sem["r_rk"], 1)
                        pool.wait_ge(sem["r_ru"], u.at("r_ru", 1))
                        q.tensor_tensor(VR[:], V_[:], RU[:].unsqueeze(1).broadcast_to([P, RS, T]), ALU.mult)\
                            .then_inc(sem["r_vr"], 1)
                        pool.wait_ge(sem["r_var"], u.at("r_var", 1))
                        inv_std(rstd[:], veps[:], small[:, 1], 1.0 / RS, T, sem["r_ystd"])
                        pool.wait_ge(sem["r_stats"], u.at("r_stats", 2))
                        inv_std(rstd[:, 0:NB], veps[:, 0:NB], mv[:, :, 1], 1.0, NB, sem["r_rstd"])

                    def attn(u):
                        for k in range(COUNTS[u.kind]["a_rstd"]):
                            pool.wait_ge(sem["a_stats"], u.at("a_stats", k + 1))
                            inv_std(arstd[:], aveps[:], amv[:, :, 1], 1.0, NB, sem["a_rstd"])
                            if k == 0:
                                pool.wait_ge(sem["mask_done"], 1)
                                if u.kind == "attn":
                                    q.tensor_copy(VA[:, :, :, AD], mcol[:].unsqueeze(2).broadcast_to([P, NB, AH]))\
                                        .then_inc(sem["a_vones"], 1)
                                else:
                                    q.memset(VA[:, :, :, AD], 1.0).then_inc(sem["a_vones"], 1)

                    rwkv(units[0])
                    attn(units[1])
                    rwkv(units[2])
                    attn(units[3])

                @block.scalar
                def _(act):
                    s = nc.scalar
                    count = [0]

                    def link(ins):
                        count[0] += 1
                        ins.then_inc(sem["s_chain"], 1)
                        act.wait_ge(sem["s_chain"], count[0])

                    def chan_norm(u, k):
                        for h in range(HALF):
                            act.wait_ge(sem["r_zT"], u.at("r_zT", 2 * k + h + 1))
                            s.activation(XN[:, h, :, 1:T + 1], PA[:, h * 512:(h + 1) * 512].rearrange("p (b t) -> p b t", b=NB),
                                         ACT.Identity, bias=r_(u.layer, "ln_b")[:, 2 * k + h:2 * k + h + 1],
                                         scale=r_(u.layer, "ln_w")[:, 2 * k + h:2 * k + h + 1]).then_inc(sem["r_xn"], 1)

                    def first_column(u, c):
                        if c >= 2:
                            act.wait_ge(sem["r_y"], u.at("r_y", c - 1))
                        s.copy(A_[c % 2][:, :, :, 0], s0_sb[:].rearrange("p k d -> p d k")[:, DC * c:DC * c + DC])\
                            .then_inc(sem["r_s0"], 1)

                    def rwkv(u):
                        chan_norm(u, 0)
                        act.wait_ge(sem["r_used"], u.at("r_used", 1))
                        s.activation(TT[:, 0], PB[:, 0:512], ACT.Tanh)
                        s.activation(TT[0:MIX, 1], PB[0:MIX, 512:1024], ACT.Tanh).then_inc(sem["r_lowrank"], 1)
                        act.wait_ge(sem["r_used"], u.at("r_used", 2))
                        s.activation(thT[0:DEC, :], PB[0:DEC, 0:512], ACT.Tanh).then_inc(sem["r_dec"], 1)
                        act.wait_ge(sem["r_turned"], u.at("r_turned", 1))
                        link(s.activation(E_[:], E_[:], ACT.Exp))
                        s.activation(W_[:, :, 1:T], E_[:, :, 0:T - 1], ACT.Exp, scale=-1.0).then_inc(sem["r_w"], 1)
                        first_column(u, 0)
                        first_column(u, 1)
                        act.wait_ge(sem["r_used"], u.at("r_used", 6))
                        s.activation(Gt[:].rearrange("p h b t -> p (h b t)"), PB[:], ACT.Tanh, scale=0.5)\
                            .then_inc(sem["r_tg"], 1)
                        for c in range(2, NCH):
                            first_column(u, c)
                        act.wait_ge(sem["r_yc"], u.at("r_yc", 1))
                        s.activation(tmp[:].rearrange("p h b t -> p (h b t)"), z[:].rearrange("p b c -> p (b c)"), ACT.Square)\
                            .then_inc(sem["r_sq"], 1)
                        for h in range(HALF):
                            act.wait_ge(sem["r_yT"], u.at("r_yT", h + 1))
                            s.activation(TT[:, h], PB[:, h * 512:(h + 1) * 512],
                                         ACT.Identity, bias=r_(u.layer, "gn_b")[:, h:h + 1], scale=r_(u.layer, "gn_w")[:, h:h + 1])\
                                .then_inc(sem["r_yn"], 1)
                        chan_norm(u, 1)
                        ef = E_[:].rearrange("p k t -> p (k t)")
                        act.wait_ge(sem["r_used"], u.at("r_used", 7))
                        link(s.activation(ef, PB[:], ACT.Relu))
                        s.activation(ef, ef, ACT.Square).then_inc(sem["r_kk"], 1)
                        act.wait_ge(sem["r_used"], u.at("r_used", 8))
                        s.activation(R_[:].rearrange("p k t -> p (k t)"), PA[:], ACT.Tanh, scale=0.5).then_inc(sem["r_rr"], 1)

                    def attn(u):
                        mlp = u.kind == "attn_mlp"

                        def norm_x(k):
                            for h in range(HALF):
                                act.wait_ge(sem["a_xT"], u.at("a_xT", 2 * k + h + 1))
                                src = bank(h + 2 * k)
                                if mlp:
                                    ins = s.activation(XT[:, h], src, ACT.Identity, bias=a_(u.layer, "ln_b")[:, 2 * k + h:2 * k + h + 1],
                                                       scale=a_(u.layer, "ln_w")[:, 2 * k + h:2 * k + h + 1])
                                else:
                                    ins = s.activation(XT[:, h], src, ACT.Copy)
                                ins.then_inc(sem["a_xc"], 1)

                        norm_x(0)
                        if not mlp:
                            for h in range(HALF):
                                act.wait_ge(sem["a_cT"], u.at("a_cT", h + 1))
                                s.activation(CT[:, h], bank(2 + h), ACT.Identity, bias=a_(u.layer, "ln_b")[:, h:h + 1],
                                             scale=a_(u.layer, "ln_w")[:, h:h + 1]).then_inc(sem["a_cc"], 1)
                        for j in range(HPQ):
                            act.wait_ge(sem["a_qk"], u.at("a_qk", HPQ + j + 1))
                            s.activation(K2[:, j], bank(j), ACT.Identity, bias=a_(u.layer, "kb")[:, j:j + 1])\
                                .then_inc(sem["a_k"], 1)
                        act.wait_ge(sem["a_vp"], u.at("a_vp", 1))
                        vp = QA[:].rearrange("p (b h d) -> p b h d", b=NB, h=AH)
                        for b in range(NB):
                            if mlp:
                                last = s.activation(VA[:, b, :, 0:AD], vp[:, b], ACT.Copy)
                            else:
                                last = s.activation(VA[:, b, :, 0:AD], vp[:, b], ACT.Copy, scale=mcol[:, b:b + 1])
                        last.then_inc(sem["a_v"], 1)
                        for n in range(NB * HPQ):
                            act.wait_ge(sem["a_max"], u.at("a_max", n + 1))
                            if n >= 2:
                                act.wait_ge(sem["a_pT"], u.at("a_pT", n - 1))
                            for j in range(HPQ):
                                last = s.activation(PR[:, n % 2, j], bank(2 + n % 2)[:, j * T:(j + 1) * T], ACT.Exp,
                                                    bias=nmax[:, n % 2, j:j + 1])
                            last.then_inc(sem["a_exp"], 1)
                        for h in range(HALF):
                            act.wait_ge(sem["a_oT"], u.at("a_oT", h + 1))
                            s.activation(CT[:, h], bank(2 + h), ACT.Copy).then_inc(sem["a_oc"], 1)
                        if mlp:
                            norm_x(1)
                            for m in range(FFT):
                                act.wait_ge(sem["a_fc"], u.at("a_fc", m + 1))
                                s.activation(H_[:, m], bank(m % 4), ACT.Gelu_apprx_tanh, bias=m_("fc_b")[:, m:m + 1])\
                                    .then_inc(sem["a_gelu"], 1)

                    act.wait_ge(sem["mask_done"], 1)
                    rwkv(units[0])
                    attn(units[1])
                    rwkv(units[2])
                    attn(units[3])

                @block.tensor
                def _(pe):
                    t = nc.tensor

                    def turn_tokens(dst, src, done):
                        for h in range(HALF):
                            for b in range(NB):
                                last = t.transpose(dst(h)[:, b * T:(b + 1) * T], src[:, b, h * P:(h + 1) * P], ident)
                            last.then_inc(done, 1)

                    def chan_proj(dst, w, src, done):
                        for m in range(HALF):
                            for h in range(HALF):
                                last = t.matmul(dst[:, m * 512:(m + 1) * 512], w[:, h, m * P:(m + 1) * P], src[:, h],
                                                start=(h == 0), stop=(h == HALF - 1))
                        last.then_inc(done, 1)

                    def token_proj(dst, w, lhs, done, bias=None):
                        for b in range(NB):
                            o = dst[:, b * C:(b + 1) * C]
                            for h in range(HALF):
                                last = t.matmul(o, lhs(h, b), w[:, h], start=(h == 0), stop=(h == HALF - 1 and bias is None))
                            if bias is not None:
                                last = t.matmul(o, ones_row, bias, start=False, stop=True)
                        last.then_inc(done, 1)

                    def rwkv(u):
                        L = u.layer
                        pa = lambda h: PA[:, h * 512:(h + 1) * 512]
                        pb = lambda h: PB[:, h * 512:(h + 1) * 512]
                        flat = lambda buf: buf[:].rearrange("p h b t -> p h (b t)")

                        def maa(f):
                            for h in range(HALF):
                                if f < 4:
                                    w2 = r_(L, "w2a")[MIX * f:MIX * f + MIX, h * P:(h + 1) * P]
                                    tt = TT[MIX * f:MIX * f + MIX, 0]
                                    pos = (MIX * f, 0)
                                else:
                                    w2 = r_(L, "w2b")[0:MIX, h * P:(h + 1) * P]
                                    tt = TT[0:MIX, 1]
                                    pos = (0, 0)
                                last = t.matmul(pa(h), w2, tt, start=True, stop=True, tile_position=pos)
                            last.then_inc(sem["r_maa"], 1)

                        pe.wait_ge(sem["r_z"], u.at("r_z", 1))
                        turn_tokens(pa, z, sem["r_zT"])
                        pe.wait_ge(sem["r_mixed"], u.at("r_mixed", 1))
                        w1 = rh_(L, "w1")
                        for h in range(HALF):
                            t.matmul(PB[:, 0:512], w1[:, h, 0:P], flat(X5[0])[:, h], start=(h == 0), stop=(h == 1))
                        for h in range(HALF):
                            last = t.matmul(PB[0:MIX, 512:1024], w1[:, h, P:P + MIX], flat(X5[0])[:, h], start=(h == 0), stop=(h == 1))
                        last.then_inc(sem["r_used"], 1)
                        pe.wait_ge(sem["r_lowrank"], u.at("r_lowrank", 1))
                        maa(0)
                        pe.wait_ge(sem["r_mixed"], u.at("r_mixed", 2))
                        maa(1)
                        dw1 = rh_(L, "dw1")
                        for h in range(HALF):
                            last = t.matmul(PB[0:DEC, 0:512], dw1[:, h], flat(X5[1])[:, h], start=(h == 0), stop=(h == 1))
                        last.then_inc(sem["r_used"], 1)
                        pe.wait_ge(sem["r_dec"], u.at("r_dec", 1))
                        for a in range(TB):
                            last = t.matmul(PB[:, a * C:(a + 1) * C],
                                            thT[0:DEC + 1, a * P:(a + 1) * P],
                                            r_(L, "dw2")[0:DEC + 1, :], start=True, stop=True)
                        last.then_inc(sem["r_decay"], 1)
                        for f, w in ((1, "Wk"), (2, "Wv"), (3, "Wr")):
                            pe.wait_ge(sem["r_mixed"], u.at("r_mixed", f + 2))
                            maa(f + 1)
                            pe.wait_ge(sem["r_turned"], u.at("r_turned", f))
                            src = flat(X5[(f + 1) % 2])
                            wt = rh_(L, w)
                            for a in range(TB):
                                for h in range(HALF):
                                    last = t.matmul(PB[:, a * C:(a + 1) * C], src[:, h, a * P:(a + 1) * P], wt[:, h],
                                                    start=(h == 0), stop=(h == HALF - 1))
                            last.then_inc(sem["r_used"], 1)
                        pe.wait_ge(sem["r_mixed"], u.at("r_mixed", 6))
                        pe.wait_ge(sem["r_turned"], u.at("r_turned", 4))
                        wg = rh_(L, "Wg")
                        for m in range(HALF):
                            for h in range(HALF):
                                last = t.matmul(pb(m), wg[:, h, m * P:(m + 1) * P], flat(X5[1])[:, h], start=(h == 0), stop=(h == 1))
                        last.then_inc(sem["r_used"], 1)
                        for c in range(NCH):
                            pe.wait_ge(sem["r_rs"], u.at("r_rs", c + 1))
                            if c == 0:
                                pe.wait_ge(sem["r_vr"], u.at("r_vr", 1))
                            o = PA[:, c * DC * T:(c + 1) * DC * T]
                            t.matmul(o, ident, VR[:, c * DC:(c + 1) * DC], start=True, stop=False)
                            for k in range(RS):
                                last = t.matmul(o, ident, A_[c % 2][:, :, k], start=False, stop=(k == RS - 1))
                            last.then_inc(sem["r_y"], 1)
                        pe.wait_ge(sem["r_yt"], u.at("r_yt", 1))
                        yt = X5[1][:].rearrange("p h b t -> p (h b t)").rearrange("p (a c) -> p a c", a=TB)
                        turn_tokens(pb, yt, sem["r_yT"])
                        pe.wait_ge(sem["r_yg"], u.at("r_yg", 1))
                        token_proj(PA, rh_(L, "Wo"), lambda h, b: SX[:, h, b], sem["r_o"])
                        pe.wait_ge(sem["r_z"], u.at("r_z", 2))
                        turn_tokens(pa, z, sem["r_zT"])
                        pe.wait_ge(sem["r_mixed"], u.at("r_mixed", 7))
                        chan_proj(PB, rh_(L, "fWk"), flat(X5[0]), sem["r_used"])
                        pe.wait_ge(sem["r_mixed"], u.at("r_mixed", 8))
                        token_proj(PA, rh_(L, "fWr"), lambda h, b: X5[1][:, h, b], sem["r_used"])
                        pe.wait_ge(sem["r_kk"], u.at("r_kk", 1))
                        kk = E_[:].rearrange("p k t -> p (k t)").rearrange("p (h b t) -> p h b t", h=HALF, b=NB)
                        token_proj(PB, rh_(L, "fWv"), lambda h, b: kk[:, h, b], sem["r_fv"])

                    def attn(u):
                        L = u.layer
                        mlp = u.kind == "attn_mlp"
                        first = 0
                        if mlp:
                            pe.wait_ge(sem["a_z"], u.at("a_z", 1))
                            turn_tokens(bank, az, sem["a_xT"])
                            pe.wait_ge(sem["ld_ctxT"], 16)
                            c_t = ctx_chan
                        else:
                            pe.wait_ge(sem["x_done"], u.at("x_done", 0))
                            turn_tokens(bank, X, sem["a_xT"])
                            pe.wait_ge(sem["a_z"], u.at("a_z", 1))
                            turn_tokens(lambda h: bank(2 + h), az, sem["a_cT"])
                            c_t = CT[:]
                        for j in range(HPQ):
                            if j == 0:
                                pe.wait_ge(sem["a_xc"], u.at("a_xc", 2))
                            if j == 2 and not mlp:
                                pe.wait_ge(sem["a_cc"], u.at("a_cc", 2))
                            for h in range(HALF):
                                last = t.matmul(bank(j), ah_(L, "Wq")[:, h, j * P:(j + 1) * P], XT[:, h], start=(h == 0), stop=(h == 1))
                            last.then_inc(sem["a_qk"], 1)
                        pe.wait_ge(sem["mask_done"], 1)
                        for j in range(HPQ):
                            pe.wait_ge(sem["a_q"], u.at("a_q", j + 1))
                            for h in range(HALF):
                                t.matmul(bank(j), ah_(L, "Wk")[:, h, j * P:(j + 1) * P], c_t[:, h], start=(h == 0), stop=False)
                            t.matmul(bank(j), maskrow_sel, mrow[0:1, :], start=False, stop=True).then_inc(sem["a_qk"], 1)
                        pe.wait_ge(sem["a_k"], u.at("a_k", 2))
                        token_proj(QA, ah_(L, "Wv"), lambda h, b: c_t[:, h, b * T:(b + 1) * T], sem["a_vp"],
                                   m_("v_b")[0:1, :] if mlp else None)

                        def scores(n):
                            b, i = divmod(n, HPQ)
                            if n == 0:
                                pe.wait_ge(sem["a_k"], u.at("a_k", HPQ))
                            if n >= 2:
                                pe.wait_ge(sem["a_exp"], u.at("a_exp", n - 1))
                            for j in range(HPQ):
                                last = t.matmul(bank(2 + n % 2)[:, j * T:(j + 1) * T], Q_[32 * i:32 * i + 32, j, b * T:(b + 1) * T],
                                                K2[32 * i:32 * i + 32, j, b * T:(b + 1) * T], start=True, stop=True,
                                                tile_position=(32 * i, 0))
                            last.then_inc(sem["a_s"], 1)

                        def probs_T(n):
                            pe.wait_ge(sem["a_exp"], u.at("a_exp", n + 1))
                            if n == 0:
                                pe.wait_ge(sem["a_v"], u.at("a_v", 1))
                            else:
                                pe.wait_ge(sem["a_pc"], u.at("a_pc", n))
                            for j in range(HPQ):
                                last = t.transpose(bank(0)[:, j * T:(j + 1) * T], PR[:, n % 2, j], ident)
                            last.then_inc(sem["a_pT"], 1)

                        def values(n):
                            b, i = divmod(n, HPQ)
                            pe.wait_ge(sem["a_pc"], u.at("a_pc", n + 1))
                            if n == 0:
                                pe.wait_ge(sem["a_vones"], u.at("a_vones", 1))
                            elif i == 0:
                                pe.wait_ge(sem["a_on"], u.at("a_on", b))
                            for j in range(HPQ):
                                head = HPQ * i + j
                                last = t.matmul(bank(1)[:, head * (AD + 1):(head + 1) * (AD + 1)], PT[:, n % 2, j], VA[:, b, head],
                                                start=True, stop=True)
                            last.then_inc(sem["a_pv"], 1)

                        jobs = NB * HPQ
                        for n in range(jobs + 2):
                            if n < jobs:
                                scores(n)
                            if 1 <= n <= jobs:
                                probs_T(n - 1)
                            if n >= 2:
                                values(n - 2)
                        pe.wait_ge(sem["a_on"], u.at("a_on", NB))
                        turn_tokens(lambda h: bank(2 + h), az, sem["a_oT"])
                        pe.wait_ge(sem["a_oc"], u.at("a_oc", 2))
                        token_proj(QA, ah_(L, "Wo"), lambda h, b: CT[:, h, b * T:(b + 1) * T], sem["a_o"],
                                   m_("o_b")[0:1, :] if mlp else None)
                        if mlp:
                            pe.wait_ge(sem["a_z"], u.at("a_z", 2))
                            turn_tokens(lambda h: bank(2 + h), az, sem["a_xT"])
                            pe.wait_ge(sem["a_xc"], u.at("a_xc", 4))
                            fc = m_("fc").rearrange("p (h n) -> p h n", h=HALF)
                            for m in range(FFT):
                                if m >= 4:
                                    pe.wait_ge(sem["a_gelu"], u.at("a_gelu", m - 3))
                                for h in range(HALF):
                                    last = t.matmul(bank(m % 4), fc[:, h, m * P:(m + 1) * P], XT[:, h], start=(h == 0), stop=(h == 1))
                                last.then_inc(sem["a_fc"], 1)
                            pe.wait_ge(sem["a_gelu"], u.at("a_gelu", FFT))
                            proj = m_("proj").rearrange("p (m n) -> p m n", m=FFT)
                            for b in range(NB):
                                o = QA[:, b * C:(b + 1) * C]
                                for m in range(FFT):
                                    t.matmul(o, H_[:, m, b * T:(b + 1) * T], proj[:, m], start=(m == 0), stop=False)
                                last = t.matmul(o, ones_row, m_("proj_b")[0:1, :], start=False, stop=True)
                            last.then_inc(sem["a_mlp"], 1)

                    rwkv(units[0])
                    attn(units[1])
                    rwkv(units[2])
                    attn(units[3])

            nc.all_engine_barrier()
            for n in names + extra[2:]:
                nc.sync.sem_clear(sem[n])
            nc.all_engine_barrier()


def kernel(**inputs):
    import numpy as np
    import concourse.bacc as _bacc
    from concourse import mybir as _mybir
    from concourse.bass_utils import run_bass_kernel_spmd as _run

    a = {k: np.ascontiguousarray(v) for k, v in inputs.items()}
    perm = np.arange(C).reshape(RH, RS).T.reshape(-1)

    def vec(v):
        return v.reshape(-1, P).T

    def mat(w):
        return w.reshape(-1, P, w.shape[1]).transpose(1, 0, 2).reshape(P, -1)

    def rows(w):
        out = np.zeros((P, w.shape[1]), w.dtype)
        out[:w.shape[0]] = w
        return out

    def quadrants(w):
        out = np.zeros((w.shape[0], HPQ, HPQ, 32), w.dtype)
        out[:, :, :, 0:AD] = w.reshape(w.shape[0], HPQ, HPQ, AD).transpose(0, 2, 1, 3)
        return mat(out.reshape(w.shape[0], HPQ * P))

    def quadrant_bias(b, extra):
        out = np.zeros((HPQ, 32, HPQ), np.float32)
        if b is not None:
            out[:, 0:AD, :] = b.reshape(HPQ, HPQ, AD).transpose(0, 2, 1)
        out[:, AD, :] = extra
        return out.reshape(P, HPQ)

    def pack(cols, parts):
        for name, n in cols:
            assert parts[name].shape == (P, n), (name, parts[name].shape, n)
        return np.ascontiguousarray(np.concatenate([parts[name] for name, _ in cols], axis=1))

    def rwkv_pack(pre, order, maa, fk, fr, fwr, fwk, fwv):
        w = lambda n: a[f"{pre}_{n}"]
        w1 = w("maa_w1").reshape(C, NMIX, MIX)[:, order].reshape(C, NMIX * MIX)
        w2 = w("maa_w2")[order]
        dw2 = np.concatenate([w("decay_w2"), w("time_decay")[None]], 0)[:, perm]
        return pack(RWKV_COLS, dict(
            w1=mat(w1), w2a=w2[0:4].reshape(P, C), w2b=rows(w2[4]), dw1=mat(w("decay_w1")), dw2=rows(dw2),
            Wr=mat(w("Wr").T[:, perm]), Wk=mat(w("Wk").T[:, perm]), Wv=mat(w("Wv").T[:, perm]),
            Wg=mat(w("Wg").T[:, perm]), Wo=mat(w("Wo").T[perm]),
            fWr=mat(w(fwr).T), fWk=mat(w(fwk).T), fWv=mat(w(fwv).T),
            ln_w=np.concatenate([vec(w("ln1_w")), vec(w("ln2_w"))], 1),
            ln_b=np.concatenate([vec(w("ln1_b")), vec(w("ln2_b"))], 1),
            maa_x=vec(w("maa_x")), maa=np.concatenate([vec(m) for m in maa], 1),
            gn_w=vec(w("gn_w")[perm]), gn_b=vec(w("gn_b")[perm]), fk=vec(w(fk)), fr=vec(w(fr)),
            u=np.tile(w("faaaa").reshape(RH, RS), (NB, 1))))

    stack = a["L0_xattn_maa_stack"]
    r0 = rwkv_pack("L0_xattn", [1, 0, 2, 3, 4], [stack[i] for i in (1, 0, 2, 3, 4)], "ffn_maa_k", "ffn_maa_r",
                   "ffn_Wr", "ffn_Wk", "ffn_Wv")
    r1 = rwkv_pack("L2_xattn", [0, 1, 2, 3, 4], [a[f"L2_xattn_maa_{n}"] for n in "wkvrg"], "fmaa_k", "fmaa_r",
                   "fWr", "fWk", "fWv")
    one = AD ** 0.5
    zero4 = np.zeros((P, 2 * HALF), np.float32)
    w = lambda n: a[f"L1_xattn_{n}"]
    a0 = pack(ATTN_COLS, dict(
        Wq=quadrants(w("Wq").T), Wk=quadrants(w("Wk").T), Wv=mat(w("Wv").T), Wo=mat(w("Wo").T),
        qb=quadrant_bias(None, one), kb=quadrant_bias(None, 0.0),
        ln_w=np.concatenate([vec(w("ln_gamma")), zero4[:, 0:HALF]], 1),
        ln_b=np.concatenate([vec(w("ln_beta")), zero4[:, 0:HALF]], 1), gate=np.tile(w("gate")[None], (P, 1))))
    w3 = lambda n: a[f"L3_xattn_{n}"]
    a1 = pack(ATTN_COLS, dict(
        Wq=quadrants(w3("q_w")), Wk=quadrants(w3("k_w")), Wv=mat(w3("v_w")), Wo=mat(w3("cproj_w")),
        qb=quadrant_bias(w3("q_b"), one), kb=quadrant_bias(w3("k_b"), 0.0),
        ln_w=np.concatenate([vec(w3("ln1_w")), vec(w3("ln2_w"))], 1),
        ln_b=np.concatenate([vec(w3("ln1_b")), vec(w3("ln2_b"))], 1), gate=zero4[:, 0:1]))
    mlp = pack(MLP_COLS, dict(fc=mat(w3("fc_w")), proj=mat(w3("proj_w")), fc_b=vec(w3("fc_b")),
                              v_b=rows(w3("v_b")[None]), o_b=rows(w3("cproj_b")[None]), proj_b=rows(w3("proj_b")[None])))
    sel = np.zeros((P, P), np.float32)
    sel[0, AD::32] = 1.0
    common = pack(COMMON_COLS, dict(ident=np.eye(P, dtype=np.float32), ones=np.ones((P, P), np.float32), maskrow=sel))

    ctx = a["ctx_2048"]
    mask = a["mask_BxS2_bf1"].view(np.uint8)
    by_token = lambda m: m.reshape(G, NB, T, C).transpose(0, 2, 1, 3)
    arrays = {
        "x": by_token(a["x"]),
        "ctx": by_token(ctx),
        "ctx_t": ctx.reshape(G, NB, T, HALF, P).transpose(0, 4, 3, 1, 2).reshape(G, P, HALF, N),
        "s0": ctx[:, 2:2 + RS].reshape(G, P, RS, RS),
        "state": ctx[:, 0:2].reshape(G, NB, 2, HALF, P).transpose(0, 4, 2, 3, 1),
        "mask_row": mask.reshape(G, 1, N),
        "mask_col": mask.reshape(G, NB, T).transpose(0, 2, 1),
        "rwkv_w": np.stack([r0, r1]),
        "attn_w": np.stack([a0, a1]),
        "mlp_w": mlp,
        "common": common,
    }
    arrays = {k: np.ascontiguousarray(v) for k, v in arrays.items()}
    nc = _bacc.Bacc("TRN2", target_bir_lowering=False, num_devices=1)
    args = [nc.dram_tensor(f"in_{k}", v.shape, _mybir.dt.from_np(v.dtype), kind="ExternalInput").ap() for k, v in arrays.items()]
    args.append(nc.dram_tensor("out_0", (G, T, NB, C), F32, kind="ExternalOutput").ap())
    build(nc, *args)
    r = _run(nc, [{f"in_{k}": v for k, v in arrays.items()}], core_ids=[0])
    return r.results[0]["out_0"].reshape(G, T, NB, C).transpose(0, 2, 1, 3).reshape(B, T, C)
```

```python
from contextlib import ExitStack

import concourse.bass as bass
from concourse import mybir

F32 = mybir.dt.float32
BF16 = mybir.dt.bfloat16
U8 = mybir.dt.uint8
ALU = mybir.AluOpType
ACT = mybir.ActivationFunctionType
AX = mybir.AxisListType

P = 128
C = 256
HALF = C // P
T = 128
B = 16
NB = 4
G = B // NB
N = NB * T
RH, RS = 32, 8
MIX, DEC = 32, 64
NMIX = 5
AH, AD = 16, 16
QUAD = 4
JH = 4
FF = 1024
FFT = FF // P
TB = T // 32
DC = 2
NCH = RS // DC
EPS = 1e-5
MASKED = 1e30

RWKV_COLS = [("w1", HALF * NMIX * MIX), ("w2a", C), ("w2b", C), ("dw1", HALF * DEC), ("dw2", C),
             ("Wr", HALF * C), ("Wk", HALF * C), ("Wv", HALF * C), ("Wg", HALF * C), ("Wo", HALF * C),
             ("fWr", HALF * C), ("fWk", HALF * C), ("fWv", HALF * C),
             ("ln_w", 2 * HALF), ("ln_b", 2 * HALF), ("maa_x", HALF), ("maa", NMIX * HALF),
             ("gn_w", HALF), ("gn_b", HALF), ("fk", HALF), ("fr", HALF), ("u", RS)]
ATTN_COLS = [("Wq", HALF * C), ("Wk", HALF * C), ("Wv", HALF * C), ("Wo", HALF * C),
             ("qb", HALF), ("kb", 2 * HALF), ("ln_w", 2 * HALF), ("ln_b", 2 * HALF), ("gate", 1)]
MLP_COLS = [("fc", HALF * FF), ("proj", FFT * C), ("fc_b", FFT)]
COMMON_COLS = [("ident", P), ("parity", 2)]
BIASES = 3


def spans(cols):
    at, out = 0, {}
    for name, n in cols:
        out[name] = (at, at + n)
        at += n
    return out, at


COUNTS = {
    "mixer": dict(r_stats=1, r_rstd=1, r_z=1, r_zT=2, r_xn=2, r_mixed=6, r_used=6, r_lowrank=1, r_maa=5,
                  r_dec=1, r_decay=1, r_turned=4, r_w=1, r_tg=1, r_rk=1, r_ru=1, r_s0=4, r_rs=4,
                  r_y=4, r_yc=1, r_sq=1, r_var=1, r_ystd=1, r_yt=1, r_yT=2, r_yn=2, r_yg=1, r_o=1, x_done=1),
    "attn": dict(a_stats=1, a_rstd=1, a_z=1, a_xT=2, a_xc=2, a_cT=2, a_cc=2, a_mask=1),
    "attn_mlp": dict(a_stats=2, a_rstd=2, a_z=2, a_xT=4, a_xc=4, a_fc=8, a_gelu=8, a_mlp=1, a_out=1),
}
for _kind in ("attn", "attn_mlp"):
    COUNTS[_kind].update(f_stats=1, f_rstd=1, f_z=1, f_zT=2, f_xn=2, f_mixed=2, f_k=1, f_kk=1, f_r=1, f_rr=1, f_v=1,
                         a_kp=2, a_qp=2, a_q=2, a_k=2, a_vp=1, a_v=1, a_vones=1, a_s=16, a_max=16, a_exp=16,
                         a_pT=16, a_pc=16, a_pv=16, a_on=4, a_oT=2, a_oc=2, a_o=1, x_done=2)
PER_LANE = ("x_done",)


class Unit:

    def __init__(self, kind, layer, lane, before):
        self.kind, self.layer, self.lane = kind, layer, lane
        self.base = {}
        self.other_x_done = sum(COUNTS[unit.kind]["x_done"] for unit in before if unit.lane != lane)
        for unit in before:
            for name, n in COUNTS[unit.kind].items():
                if name not in PER_LANE or unit.lane == lane:
                    self.base[name] = self.base.get(name, 0) + n

    def at(self, name, n):
        return self.base.get(name, 0) + n


ORDER = {
    "attn": {
        "VectorE": "AMAMAMAMAAAAMAMMMAMMMAMAMMAMMAMMAAAMAMMAMAAAMMAMAAMAMAAMAMMA",
        "GpSimd": "AMAMMMMMM",
        "ScalarE": "AMAMAMAAMAAAAAAMAAAAAAAAAAAMAAAAAMAAAAAAAAMAAAAMAMA",
        "TensorE": "AMAMAMAMMAMAAAMAMAMMAMMAAAMAAAAAAAAAAAAAAAAAAAAAAAAAAAAAAAMAMA",
    },
    "attn_mlp": {
        "VectorE": "MAMAMAAMMAMAAMAMAMAAMAMMAAAAAMAMAMAAAMAMAMMAAMAAMMAMMAAMMMMMMA",
        "GpSimd": "MAAMMMMMAM",
        "ScalarE": "AAAMAMAAMAAAAMAAAAAAAAMAAAAAAAAAAAAAAAMAAAAAMAAAAAAMAMAAAAM",
        "TensorE": "AAMAMAMAMMAMMMAMAMAAMAAAMAAAAAAAAMAAAAAAAAAAAAAAAAAAAAAAAAAAAAAAAAAAMAAAMA",
    },
}


def in_order(engine, slot, mixer, attn):
    programs = {"M": mixer(slot[0])}
    order = None
    if len(slot) > 1:
        programs["A"] = attn(slot[1])
        order = ORDER[slot[1].kind][engine]
    for program in programs.values():
        next(program)
    if order:
        for letter in order:
            next(programs[letter], None)
    for program in programs.values():
        assert order is None or next(program, "done") == "done"
        for _ in program:
            pass


def build(nc, x, ctx, ctx_t, s0, state, mask_row, mask_col, rwkv_w, attn_w, mlp_w, bias_w, common, out):
    rw, rw_n = spans(RWKV_COLS)
    aw, aw_n = spans(ATTN_COLS)
    mw, mw_n = spans(MLP_COLS)
    cw, cw_n = spans(COMMON_COLS)

    with ExitStack() as stack:
        def sb(name, shape, dt=F32):
            return stack.enter_context(nc.sbuf_tensor(name, [P] + shape, dt))

        r_pack = [sb(f"rwkv_w{i}", [rw_n]) for i in range(2)]
        a_pack = [sb(f"attn_w{i}", [aw_n]) for i in range(2)]
        m_pack = sb("mlp_w", [mw_n])
        c_pack = sb("common_w", [cw_n])
        tanh_gate = sb("tanh_gate", [1])
        half_pow = sb("half_pow", [NB])

        def r_(layer, name):
            return r_pack[layer][:, rw[name][0]:rw[name][1]]

        def rh_(layer, name):
            return r_(layer, name).rearrange("p (h n) -> p h n", h=HALF)

        def a_(layer, name):
            return a_pack[layer][:, aw[name][0]:aw[name][1]]

        def ah_(layer, name):
            return a_(layer, name).rearrange("p (h n) -> p h n", h=HALF)

        def m_(name):
            return m_pack[:, mw[name][0]:mw[name][1]]

        def c_(name):
            return c_pack[:, cw[name][0]:cw[name][1]]

        ident = c_("ident")
        ones = sb("ones", [P], BF16)
        bias3_sb = sb("bias3", [BIASES, C], BF16)
        bias3 = bias3_sb[0:3]
        eps_col = sb("eps_col", [1])

        X2 = [sb(f"X_{n}", [NB, C]) for n in range(2)]
        ctx_sb = [sb(f"ctx_{n}", [NB * C]) for n in range(2)]
        ctx_tok = [c[:].rearrange("p (b c) -> p b c", b=NB) for c in ctx_sb]
        ctx_chan = [c[:].rearrange("p (h n) -> p h n", h=HALF) for c in ctx_sb]
        s0_sb = [sb(f"s0_{n}", [RS, RS]) for n in range(2)]
        st_sb = [sb(f"st_{n}", [2, HALF, NB]) for n in range(2)]
        mrow8 = sb("mrow8", [N], U8)
        mrow = [sb(f"mrow_{n}", [N], BF16) for n in range(2)]
        mcol8 = sb("mcol8", [NB], U8)
        mcol = [sb(f"mcol_{n}", [NB]) for n in range(2)]

        z = sb("z", [NB, C])
        XN = sb("XN", [HALF, NB, T + 1])
        SX = sb("SX", [HALF, NB, T])
        X5 = [sb(f"X5_{i}", [HALF, NB, T]) for i in range(2)]
        tmp = sb("tmp", [HALF, NB, T])
        thT = sb("thT", [N])
        W_ = sb("W_", [RS, T])
        K_ = sb("K_", [RS, T])
        V_ = sb("V_", [RS, T])
        R_ = sb("R_", [RS, T])
        RU = sb("RU", [T])
        A_ = [sb(f"A_{i}", [DC, RS, T]) for i in range(2)]
        S_ = sb("S_", [DC, RS, T])
        TT = S_[:, 0].rearrange("p k t -> p (k t)").rearrange("p (a n) -> p a n", a=2)
        bias_f = S_[:, 0].rearrange("p k t -> p (k t)")[:, 0:BIASES * C]
        bias_parts = A_[0][:].rearrange("p d k t -> p (d k t)").bitcast(BF16)[:, 0:3 * BIASES * C]\
            .rearrange("p (i n) -> p i n", i=3)
        Gt = sb("Gt", [HALF, NB, T])
        YT = z[:].rearrange("p b c -> p (b c)").rearrange("p (d t) -> p d t", d=RS)
        VR = SX[:].rearrange("p h b t -> p (h b) t")
        E_ = Gt[:].rearrange("p h b t -> p (h b) t")
        small = sb("small", [2, T])
        bn = sb("bn", [NB, 6])
        mv = sb("mv", [NB, 2])
        veps = sb("veps", [NB])
        rstd = sb("rstd", [T])

        az = sb("az", [NB, C])
        XT = sb("XT", [HALF, N])
        CT = sb("CT", [HALF, N])
        result = XT[:].rearrange("p h n -> p (h n)").rearrange("p (b c) -> p b c", b=NB)
        big = sb("big", [FFT, N])
        Q_ = big[:, 0:2]
        K2 = big[:, 2:6].rearrange("p (e h) n -> p e h n", e=2)
        PR = big[:, 6:8].rearrange("p a (j s) -> p a j s", j=JH)
        H_ = big
        CN = sb("CN", [HALF, NB, T + 1])
        by_seq = lambda ap: ap.rearrange("p h (b t) -> p h b t", b=NB)
        CS = by_seq(CT[:])
        C5 = [by_seq(XT[:]), by_seq(Q_)]
        CK = by_seq(big[:, 6:8])
        CR = XT[:].rearrange("p h n -> p (h n)")
        VA = sb("VA", [NB, AH, AD + 1])
        PT = XT[:].rearrange("p h n -> p (h n)").rearrange("p (a j t) -> p a j t", a=2, j=JH)
        nmax = sb("nmax", [2, JH])
        rden = sb("rden", [AH])
        abn = sb("abn", [NB, 6])
        amv = sb("amv", [NB, 2])
        aveps = sb("aveps", [NB])
        arstd = sb("arstd", [NB])

        PA = stack.enter_context(nc.psum_tensor("PA", [P, 1024], F32))
        PB = stack.enter_context(nc.psum_tensor("PB", [P, 1024], F32))
        QA = stack.enter_context(nc.psum_tensor("QA", [P, 1024], F32))
        QB = stack.enter_context(nc.psum_tensor("QB", [P, 1024], F32))

        def blocks(buf):
            return buf[:].rearrange("p h b t -> p h (b t)").rearrange("p h (a b t) -> p h a b t", a=TB, b=NB)

        def bias_rows(k):
            return bias3[:, k]

        def bank(i):
            return (QA if i < 2 else QB)[:, (i % 2) * 512:(i % 2 + 1) * 512]

        names = sorted({n for k in COUNTS.values() for n in k if n not in PER_LANE})
        sem = {n: stack.enter_context(nc.semaphore(n)) for n in names}
        lane_sem = {n: [stack.enter_context(nc.semaphore(f"{n}_{i}")) for i in range(2)]
                    for n in ("x_done", "ld_x", "ld_ctx", "ld_ctx_t", "ld_small")}
        extra = ["ld_mask", "st_out", "v_chain", "p_chain", "s_chain"]
        for n in extra + ["loaded_w", "loaded_r", "pool_setup", "bias_setup", "bias_moved"]:
            sem[n] = stack.enter_context(nc.semaphore(n))

        JOBS = NB * QUAD

        with nc.Block() as block:
            @block.sync
            def _(sp):
                sp.dma_start(bias_f[0:1, :], bias_w).then_inc(sem["bias_moved"], 16)
                sp.dma_start(c_pack[:], common).then_inc(sem["loaded_w"], 16)
                sp.wait_ge(sem["bias_setup"], 6)
                for i in range(3):
                    sp.dma_start(bias3[i:i + 1].rearrange("p k c -> p (k c)"), bias_parts[0:1, i]).then_inc(sem["bias_moved"], 16)
                sp.wait_ge(sem["loaded_w"], 16)
                sp.wait_ge(sem["bias_moved"], 64)

            @block.gpsimd
            def _(pool):
                nc.gpsimd.memset(half_pow[:], -0.5).then_inc(sem["pool_setup"], 1)
                pool.wait_ge(sem["pool_setup"], 1)
                nc.gpsimd.memset(thT[DEC:DEC + 1, :], 1.0).then_inc(sem["pool_setup"], 1)
                pool.wait_ge(sem["pool_setup"], 2)
                nc.gpsimd.memset(W_[:, :, 0:1], 0.0)

            @block.vector
            def _(dve):
                nc.vector.memset(ones[:], 1.0)
                nc.vector.memset(eps_col[:], EPS)
                f, parts = bias_f[0:1, :], [bias_parts[0:1, i] for i in range(3)]
                dve.wait_ge(sem["bias_moved"], 16)
                steps = 0
                for i in range(3):
                    steps += 1
                    nc.vector.tensor_copy(parts[i], f).then_inc(sem["bias_setup"], 1)
                    dve.wait_ge(sem["bias_setup"], steps)
                    steps += 1
                    nc.vector.tensor_tensor(f, f, parts[i], ALU.subtract).then_inc(sem["bias_setup"], 1)
                    dve.wait_ge(sem["bias_setup"], steps)

        def mixing(layer, lane, before):
            return Unit("mixer", layer, lane, before)

        def attention(layer, lane, before):
            return Unit("attn_mlp" if layer else "attn", layer, lane, before)

        def program(slots, load_first, g):
            with nc.Block() as block:
                @block.sync
                def _(sp):
                    def load(lane, group):
                        sp.dma_start(X2[lane][:], x[group]).then_inc(lane_sem["ld_x"][lane], 16)
                        sp.dma_start(st_sb[lane][:], state[group]).then_inc(lane_sem["ld_small"][lane], 16)
                        sp.dma_start(s0_sb[lane][:], s0[group]).then_inc(lane_sem["ld_small"][lane], 16)
                        sp.dma_start(ctx_tok[lane], ctx[group]).then_inc(lane_sem["ld_ctx"][lane], 16)

                    if load_first:
                        sp.dma_start(X2[0][:], x[0]).then_inc(lane_sem["ld_x"][0], 16)
                        sp.dma_start(st_sb[0][:], state[0]).then_inc(lane_sem["ld_small"][0], 16)
                        sp.dma_start(s0_sb[0][:], s0[0]).then_inc(lane_sem["ld_small"][0], 16)
                        sp.dma_start(r_pack[0][:], rwkv_w[0]).then_inc(sem["loaded_r"], 16)
                        sp.dma_start(ctx_tok[0], ctx[0]).then_inc(lane_sem["ld_ctx"][0], 16)
                        for pack, src in ((a_pack[0], attn_w[0]), (r_pack[1], rwkv_w[1]), (a_pack[1], attn_w[1]), (m_pack, mlp_w)):
                            sp.dma_start(pack[:], src).then_inc(sem["loaded_w"], 16)
                        sp.wait_ge(sem["loaded_w"], 80)
                        sp.wait_ge(lane_sem["ld_ctx"][0], 16)
                        sp.wait_ge(lane_sem["ld_small"][0], 32)
                        return
                    load(1, 2 * g + 1)
                    a0x, a0y, a1x, a1y = [a for _, a in slots]
                    for lane, unit in ((0, a0x), (1, a0y)):
                        if lane:
                            sp.wait_ge(sem["a_mask"], a0x.at("a_mask", 1))
                        sp.dma_start(mrow8[:], mask_row[2 * g + lane]).then_inc(sem["ld_mask"], 16)
                        sp.dma_start(mcol8[:], mask_col[2 * g + lane]).then_inc(sem["ld_mask"], 16)
                    for lane, unit in ((0, a0x), (1, a0y)):
                        sp.wait_ge(sem["a_z"], unit.at("a_z", 1))
                        sp.dma_start(ctx_chan[lane], ctx_t[2 * g + lane]).then_inc(lane_sem["ld_ctx_t"][lane], 16)
                    for lane, unit in ((0, a1x), (1, a1y)):
                        sp.wait_ge(sem["a_out"], unit.at("a_out", 1))
                        sp.dma_start(out[2 * g + lane], result).then_inc(sem["st_out"], 16)
                        if lane == 0:
                            load(0, 2 * g + 2)
                    sp.wait_ge(sem["st_out"], 32)
                    sp.wait_ge(lane_sem["ld_ctx"][0], 16)

                @block.vector
                def _(dve):
                    v = nc.vector
                    count = [0]

                    def link(ins):
                        count[0] += 1
                        ins.then_inc(sem["v_chain"], 1)
                        dve.wait_ge(sem["v_chain"], count[0])

                    def norm_stats(src, st, mean_var, done):
                        for b in range(NB):
                            last = v.bn_stats(st[:, b, :], src[:, b, :])
                        link(last)
                        for b in range(NB):
                            last = v.bn_aggr(mean_var[:, b, :], st[:, b, :])
                        last.then_inc(done, 1)

                    def norm_apply(dst, src, mean_var, rs, done):
                        for b in range(NB):
                            last = v.tensor_scalar(dst[:, b, :], src[:, b, :], mean_var[:, b, 0:1], rs[:, b:b + 1],
                                                   ALU.subtract, ALU.mult)
                        last.then_inc(done, 1)

                    def x_ready(u, n):
                        if u.at("x_done", n):
                            dve.wait_ge(lane_sem["x_done"][u.lane], u.at("x_done", n))

                    def mix(dst, xn, sx, vec, done):
                        for h in range(HALF):
                            last = v.scalar_tensor_tensor(dst[:, h], sx[:, h], vec[:, h:h + 1], xn[:, h, :, 1:T + 1],
                                                          ALU.mult, ALU.add)
                        last.then_inc(done, 1)

                    def mix_low_rank(u, f):
                        dve.wait_ge(sem["r_maa"], u.at("r_maa", f + 1))
                        use = f + 1
                        for h in range(HALF):
                            col = rw["maa"][0] + f * HALF + h
                            last = v.scalar_tensor_tensor(tmp[:, h], PA[:, h * 512:(h + 1) * 512].rearrange("p (b t) -> p b t", b=NB),
                                                          r_pack[u.layer][:, col:col + 1], SX[:, h], ALU.add, ALU.mult)
                        link(last)
                        if use >= 2:
                            dve.wait_ge(sem["r_used"], u.at("r_used", use - 1))
                        split = lambda ap: ap.rearrange("p b (a t) -> p a b t", a=TB)
                        for h in range(HALF):
                            last = v.tensor_tensor(blocks(X5[use % 2])[:, h], split(tmp[:, h]), split(XN[:, h, :, 1:T + 1]), ALU.add)
                        last.then_inc(sem["r_mixed"], 1)

                    def turn(u, n, dst):
                        if n == 0:
                            dve.wait_ge(sem["r_decay"], u.at("r_decay", 1))
                        else:
                            dve.wait_ge(sem["r_used"], u.at("r_used", n + 2))
                        v.transpose(dst.rearrange("p k (a t) -> p a k t", a=TB),
                                    PB[:].rearrange("p (a k h) -> p a k h", a=TB, h=32))\
                            .then_inc(sem["r_turned"], 1)

                    def outer(u, c):
                        if c >= 2:
                            dve.wait_ge(sem["r_y"], u.at("r_y", c - 1))
                        return v.tensor_tensor(A_[c % 2][:, :, :, 1:T],
                                        K_[:, :, 0:T - 1].unsqueeze(1).broadcast_to([P, DC, RS, T - 1]),
                                        V_[:, DC * c:DC * c + DC, 0:T - 1].unsqueeze(2).broadcast_to([P, DC, RS, T - 1]),
                                        ALU.mult)

                    def mixer(u):
                        xf = X2[u.lane][:].rearrange("p b c -> p (b c)")
                        yield
                        if u.layer == 0:
                            dve.wait_ge(lane_sem["ld_x"][u.lane], 16)
                            dve.wait_ge(lane_sem["ld_small"][u.lane], 32)
                        x_ready(u, 0)
                        norm_stats(X2[u.lane], bn, mv, sem["r_stats"])
                        yield
                        dve.wait_ge(sem["r_rstd"], u.at("r_rstd", 1))
                        v.tensor_copy(XN[:, :, :, 0], st_sb[u.lane][:, 1])
                        norm_apply(z, X2[u.lane], mv, rstd, sem["r_z"])
                        yield
                        dve.wait_ge(sem["r_xn"], u.at("r_xn", 2))
                        link(v.tensor_tensor(SX[:], XN[:, :, :, 0:T], XN[:, :, :, 1:T + 1], ALU.subtract))
                        if load_first:
                            dve.wait_ge(sem["loaded_r"], 16)
                        mix(X5[0], XN, SX, r_(u.layer, "maa_x"), sem["r_mixed"])
                        yield
                        mix_low_rank(u, 0)
                        yield
                        mix_low_rank(u, 1)
                        yield
                        turn(u, 0, E_)
                        yield
                        mix_low_rank(u, 2)
                        yield
                        turn(u, 1, K_[:])
                        yield
                        mix_low_rank(u, 3)
                        yield
                        turn(u, 2, V_[:])
                        yield
                        mix_low_rank(u, 4)
                        link(outer(u, 0))
                        yield
                        turn(u, 3, R_[:])
                        yield
                        dve.wait_ge(sem["r_tg"], u.at("r_tg", 1))
                        g_flat = Gt[:].rearrange("p h b t -> p (h b t)")
                        link(v.scalar_tensor_tensor(g_flat, g_flat, 1.0, PB[:], ALU.add, ALU.mult))
                        yield
                        link(outer(u, 1))
                        by_index = tmp[:].rearrange("p h b t -> p (h b) t").rearrange("p k t -> p t k")
                        yield
                        dve.wait_ge(sem["r_rk"], u.at("r_rk", 1))
                        v.tensor_reduce(RU[:], by_index, AX.X, ALU.add).then_inc(sem["r_ru"], 1)
                        for c in range(NCH):
                            yield
                            dve.wait_ge(sem["r_s0"], u.at("r_s0", c + 1))
                            if c == 0:
                                dve.wait_ge(sem["r_w"], u.at("r_w", 1))
                            else:
                                dve.wait_ge(sem["r_rs"], u.at("r_rs", c))
                            for d in range(DC):
                                last = v.tensor_tensor_scan(S_[:, d].rearrange("p k t -> p (k t)"), W_[:].rearrange("p k t -> p (k t)"),
                                                            A_[c % 2][:, d].rearrange("p k t -> p (k t)"), 0.0, ALU.mult, ALU.add)
                            link(last)
                            yield
                            v.tensor_tensor(A_[c % 2][:], R_[:].unsqueeze(1).broadcast_to([P, DC, RS, T]), S_[:], ALU.mult)\
                                .then_inc(sem["r_rs"], 1)
                            if 1 <= c < NCH - 1:
                                yield
                                link(outer(u, c + 1))
                        yield
                        dve.wait_ge(sem["r_y"], u.at("r_y", NCH))
                        link(v.tensor_reduce(small[:, 0], YT.rearrange("p d t -> p t d"), AX.X, ALU.add))
                        v.scalar_tensor_tensor(YT, small[:, 0].unsqueeze(1).broadcast_to([P, RS, T]), -1.0 / RS, YT,
                                               ALU.mult, ALU.add).then_inc(sem["r_yc"], 1)
                        yield
                        dve.wait_ge(sem["r_sq"], u.at("r_sq", 1))
                        v.tensor_reduce(small[:, 1], by_index, AX.X, ALU.add).then_inc(sem["r_var"], 1)
                        yield
                        dve.wait_ge(sem["r_ystd"], u.at("r_ystd", 1))
                        link(v.reciprocal(rstd[:], rstd[:]))
                        yn = X5[0][:].rearrange("p h b t -> p (h b) t")
                        link(v.tensor_tensor(yn, YT, rstd[:].unsqueeze(1).broadcast_to([P, RS, T]), ALU.mult))
                        v.transpose(X5[1][:].rearrange("p h b t -> p (h b t)").rearrange("p (a d h) -> p a d h", a=TB, d=RS),
                                    yn.rearrange("p d (a t) -> p a d t", a=TB)).then_inc(sem["r_yt"], 1)
                        yield
                        dve.wait_ge(sem["r_yn"], u.at("r_yn", 2))
                        for h in range(HALF):
                            last = v.tensor_tensor(SX[:, h].rearrange("p b (a t) -> p a b t", a=TB),
                                                   TT[:, h].rearrange("p (a b t) -> p a b t", a=TB, b=NB), blocks(Gt)[:, h], ALU.mult)
                        last.then_inc(sem["r_yg"], 1)
                        yield
                        dve.wait_ge(sem["r_o"], u.at("r_o", 1))
                        v.scalar_tensor_tensor(xf, PA[:], 0.5, xf, ALU.mult, ALU.add).then_inc(lane_sem["x_done"][u.lane], 1)

                    def attn(u):
                        mlp = u.kind == "attn_mlp"
                        X = X2[u.lane]
                        xf = X[:].rearrange("p b c -> p (b c)")
                        src = X if mlp else ctx_tok[u.lane]
                        yield
                        x_ready(u, 0)
                        norm_stats(X, abn, amv, sem["f_stats"])
                        yield
                        dve.wait_ge(sem["f_rstd"], u.at("f_rstd", 1))
                        v.tensor_copy(CN[:, :, :, 0], st_sb[u.lane][:, 0])
                        norm_apply(az, X, amv, arstd, sem["f_z"])
                        yield
                        dve.wait_ge(sem["f_xn"], u.at("f_xn", 2))
                        link(v.tensor_tensor(CS, CN[:, :, :, 0:T], CN[:, :, :, 1:T + 1], ALU.subtract))
                        if mlp and u.lane:
                            dve.wait_ge(sem["st_out"], 16)
                        mix(C5[0], CN, CS, r_(u.layer, "fk"), sem["f_mixed"])
                        yield
                        mix(C5[1], CN, CS, r_(u.layer, "fr"), sem["f_mixed"])
                        yield
                        dve.wait_ge(sem["f_rr"], u.at("f_rr", 1))
                        dve.wait_ge(sem["f_v"], u.at("f_v", 1))
                        cf = CT[:].rearrange("p h n -> p (h n)")
                        link(v.scalar_tensor_tensor(cf, CR, 1.0, QB[:], ALU.add, ALU.mult))
                        v.scalar_tensor_tensor(xf, cf, 0.5, xf, ALU.mult, ALU.add).then_inc(lane_sem["x_done"][u.lane], 1)
                        yield
                        if not mlp:
                            if u.lane:
                                dve.wait_ge(lane_sem["ld_ctx"][1], 16)
                            dve.wait_ge(sem["ld_mask"], 32 * (u.lane + 1))
                            v.tensor_scalar(mrow[u.lane][:], mrow8[:], 1.0, MASKED, ALU.subtract, ALU.mult)
                            v.tensor_copy(mcol[u.lane][:], mcol8[:]).then_inc(sem["a_mask"], 1)
                        if mlp:
                            x_ready(u, 1)
                        norm_stats(src, abn, amv, sem["a_stats"])
                        yield
                        dve.wait_ge(sem["a_rstd"], u.at("a_rstd", 1))
                        norm_apply(az, src, amv, arstd, sem["a_z"])
                        for h in range(HALF):
                            yield
                            dve.wait_ge(sem["a_qp"], u.at("a_qp", h + 1))
                            v.tensor_scalar(Q_[:, h], bank(h), a_(u.layer, "qb")[:, h:h + 1], AD ** -0.5, ALU.add, ALU.mult)\
                                .then_inc(sem["a_q"], 1)

                        def biggest(n):
                            dve.wait_ge(sem["a_s"], u.at("a_s", n + 1))
                            v.tensor_reduce(nmax[:, n % 2], bank(2 + n % 2).rearrange("p (j s) -> p j s", j=JH), AX.X,
                                            ALU.max, negate=True).then_inc(sem["a_max"], 1)

                        def normalise(b):
                            dve.wait_ge(sem["a_pv"], u.at("a_pv", QUAD * (b + 1)))
                            o = bank(1)[:, 0:AH * (AD + 1)].rearrange("p (h d) -> p h d", h=AH)
                            link(v.reciprocal(rden[:], o[:, :, AD]))
                            v.tensor_tensor(az[:, b].rearrange("p (h d) -> p h d", h=AH), o[:, :, 0:AD],
                                            rden[:].unsqueeze(2).broadcast_to([P, AH, AD]), ALU.mult)\
                                .then_inc(sem["a_on"], 1)

                        for n in range(JOBS + 2):
                            if n < JOBS:
                                yield
                                biggest(n)
                            if n >= 2 and (n - 2) % QUAD == QUAD - 1:
                                yield
                            if n >= 2 and (n - 2) % QUAD == QUAD - 1:
                                normalise((n - 2) // QUAD)
                        yield
                        dve.wait_ge(sem["a_o"], u.at("a_o", 1))
                        x_ready(u, 1)
                        if mlp:
                            v.tensor_tensor(xf, QA[:], xf, ALU.add).then_inc(lane_sem["x_done"][u.lane], 1)
                        else:
                            v.scalar_tensor_tensor(xf, QA[:], tanh_gate[:, 0:1], xf, ALU.mult, ALU.add)\
                                .then_inc(lane_sem["x_done"][u.lane], 1)
                        if not mlp:
                            return
                        x_ready(u, 2)
                        norm_stats(X, abn, amv, sem["a_stats"])
                        yield
                        dve.wait_ge(sem["a_rstd"], u.at("a_rstd", 2))
                        norm_apply(az, X, amv, arstd, sem["a_z"])
                        yield
                        dve.wait_ge(sem["a_mlp"], u.at("a_mlp", 1))
                        v.tensor_tensor(result.rearrange("p b c -> p (b c)"), QA[:], xf, ALU.add).then_inc(sem["a_out"], 1)

                    for slot in slots:
                        in_order("VectorE", slot, mixer, attn)

                @block.gpsimd
                def _(pool):
                    q = nc.gpsimd
                    count = [0]

                    def link(ins):
                        count[0] += 1
                        ins.then_inc(sem["p_chain"], 1)
                        pool.wait_ge(sem["p_chain"], count[0])

                    def inv_std(dst, scratch, var, scale, width, done):
                        link(q.tensor_scalar(scratch, var, scale, EPS, ALU.mult, ALU.add))
                        q.tensor_tensor(dst, scratch, half_pow[:, 0:width], ALU.pow).then_inc(done, 1)

                    def mixer(u):
                        yield
                        pool.wait_ge(sem["r_stats"], u.at("r_stats", 1))
                        inv_std(rstd[:, 0:NB], veps[:], mv[:, :, 1], 1.0, NB, sem["r_rstd"])
                        yield
                        pool.wait_ge(sem["r_turned"], u.at("r_turned", 4))
                        rk = tmp[:].rearrange("p h b t -> p (h b) t")
                        link(q.tensor_tensor(rk, R_[:], K_[:], ALU.mult))
                        q.tensor_tensor(rk, rk, r_(u.layer, "u").unsqueeze(2).broadcast_to([P, RS, T]), ALU.mult)\
                            .then_inc(sem["r_rk"], 1)
                        yield
                        pool.wait_ge(sem["r_ru"], u.at("r_ru", 1))
                        link(q.tensor_tensor(VR, V_[:], RU[:].unsqueeze(1).broadcast_to([P, RS, T]), ALU.mult))
                        for c in range(NCH):
                            yield
                            pool.wait_ge(sem["r_rs"], u.at("r_rs", c + 1))
                            A, y = A_[c % 2], YT[:, DC * c:DC * c + DC]
                            k = RS // 2
                            while k > 1:
                                link(q.tensor_tensor(A[:, :, 0:k], A[:, :, 0:k], A[:, :, k:2 * k], ALU.add))
                                k //= 2
                            link(q.tensor_tensor(y, A[:, :, 0], A[:, :, 1], ALU.add))
                            q.tensor_tensor(y, y, VR[:, DC * c:DC * c + DC], ALU.add).then_inc(sem["r_y"], 1)

                    def attn(u):
                        yield
                        pool.wait_ge(sem["f_stats"], u.at("f_stats", 1))
                        inv_std(arstd[:], aveps[:], amv[:, :, 1], 1.0, NB, sem["f_rstd"])
                        for k in range(COUNTS[u.kind]["a_rstd"]):
                            yield
                            pool.wait_ge(sem["a_stats"], u.at("a_stats", k + 1))
                            inv_std(arstd[:], aveps[:], amv[:, :, 1], 1.0, NB, sem["a_rstd"])
                            if k == 0:
                                if u.kind == "attn":
                                    pool.wait_ge(sem["a_mask"], u.at("a_mask", 1))
                                    q.tensor_copy(VA[:, :, :, AD], mcol[u.lane][:].unsqueeze(2).broadcast_to([P, NB, AH]))\
                                        .then_inc(sem["a_vones"], 1)
                                else:
                                    q.memset(VA[:, :, :, AD], 1.0).then_inc(sem["a_vones"], 1)

                    for slot in slots:
                        in_order("GpSimd", slot, mixer, attn)

                @block.scalar
                def _(act):
                    s = nc.scalar
                    count = [0]

                    def link(ins):
                        count[0] += 1
                        ins.then_inc(sem["s_chain"], 1)
                        act.wait_ge(sem["s_chain"], count[0])

                    def chan_norm(u, k, dst, src, zT, done):
                        for h in range(HALF):
                            act.wait_ge(sem[zT], u.at(zT, h + 1))
                            s.activation(dst[:, h, :, 1:T + 1], src[:, h * 512:(h + 1) * 512].rearrange("p (b t) -> p b t", b=NB),
                                         ACT.Identity, bias=r_(u.layer, "ln_b")[:, 2 * k + h:2 * k + h + 1],
                                         scale=r_(u.layer, "ln_w")[:, 2 * k + h:2 * k + h + 1]).then_inc(sem[done], 1)

                    def first_column(u, c):
                        if c >= 2:
                            act.wait_ge(sem["r_y"], u.at("r_y", c - 1))
                        elif c == 0 and u.layer == 0:
                            act.wait_ge(lane_sem["ld_small"][u.lane], 32)
                        s.copy(A_[c % 2][:, :, :, 0], s0_sb[u.lane][:].rearrange("p k d -> p d k")[:, DC * c:DC * c + DC])\
                            .then_inc(sem["r_s0"], 1)

                    def mixer(u):
                        yield
                        if load_first:
                            act.wait_ge(sem["loaded_r"], 16)
                        chan_norm(u, 0, XN, PA, "r_zT", "r_xn")
                        yield
                        act.wait_ge(sem["r_used"], u.at("r_used", 1))
                        s.activation(TT[:, 0], PB[:, 0:512], ACT.Tanh)
                        s.activation(TT[0:MIX, 1], PB[0:MIX, 512:1024], ACT.Tanh).then_inc(sem["r_lowrank"], 1)
                        yield
                        act.wait_ge(sem["r_used"], u.at("r_used", 2))
                        s.activation(thT[0:DEC, :], PB[0:DEC, 0:512], ACT.Tanh).then_inc(sem["r_dec"], 1)
                        yield
                        act.wait_ge(sem["r_turned"], u.at("r_turned", 1))
                        link(s.activation(E_, E_, ACT.Exp))
                        s.activation(W_[:, :, 1:T], E_[:, :, 0:T - 1], ACT.Exp, scale=-1.0).then_inc(sem["r_w"], 1)
                        first_column(u, 0)
                        first_column(u, 1)
                        yield
                        act.wait_ge(sem["r_used"], u.at("r_used", 6))
                        act.wait_ge(sem["r_w"], u.at("r_w", 1))
                        s.activation(Gt[:].rearrange("p h b t -> p (h b t)"), PB[:], ACT.Tanh, scale=0.5)\
                            .then_inc(sem["r_tg"], 1)
                        for c in range(2, NCH):
                            yield
                            first_column(u, c)
                        yield
                        act.wait_ge(sem["r_yc"], u.at("r_yc", 1))
                        s.activation(tmp[:].rearrange("p h b t -> p (h b t)"), z[:].rearrange("p b c -> p (b c)"), ACT.Square)\
                            .then_inc(sem["r_sq"], 1)
                        yield
                        act.wait_ge(sem["r_var"], u.at("r_var", 1))
                        s.activation(rstd[:], small[:, 1], ACT.Sqrt, bias=eps_col[:], scale=1.0 / RS).then_inc(sem["r_ystd"], 1)
                        yield
                        for h in range(HALF):
                            act.wait_ge(sem["r_yT"], u.at("r_yT", h + 1))
                            s.activation(TT[:, h], PB[:, h * 512:(h + 1) * 512],
                                         ACT.Identity, bias=r_(u.layer, "gn_b")[:, h:h + 1], scale=r_(u.layer, "gn_w")[:, h:h + 1])\
                                .then_inc(sem["r_yn"], 1)
                    def attn(u):
                        mlp = u.kind == "attn_mlp"

                        def norm_x(k):
                            for h in range(HALF):
                                act.wait_ge(sem["a_xT"], u.at("a_xT", 2 * k + h + 1))
                                src = bank(h + 2 * k)
                                if mlp:
                                    ins = s.activation(XT[:, h], src, ACT.Identity, bias=a_(u.layer, "ln_b")[:, 2 * k + h:2 * k + h + 1],
                                                       scale=a_(u.layer, "ln_w")[:, 2 * k + h:2 * k + h + 1])
                                else:
                                    ins = s.activation(XT[:, h], src, ACT.Copy)
                                ins.then_inc(sem["a_xc"], 1)

                        def keys_values():
                            for h in range(HALF):
                                yield
                                act.wait_ge(sem["a_kp"], u.at("a_kp", h + 1))
                                for e in range(2):
                                    last = s.activation(K2[:, e, h], bank(2 + h), ACT.Identity, bias=a_(u.layer, "kb")[:, 2 * e + h:2 * e + h + 1],
                                                        scale=c_("parity")[:, e:e + 1])
                                last.then_inc(sem["a_k"], 1)
                            yield
                            act.wait_ge(sem["a_vp"], u.at("a_vp", 1))
                            vp = QA[:].rearrange("p (b h d) -> p b h d", b=NB, h=AH)
                            if not mlp:
                                act.wait_ge(sem["a_mask"], u.at("a_mask", 1))
                            for b in range(NB):
                                if mlp:
                                    last = s.activation(VA[:, b, :, 0:AD], vp[:, b], ACT.Copy)
                                else:
                                    last = s.activation(VA[:, b, :, 0:AD], vp[:, b], ACT.Copy, scale=mcol[u.lane][:, b:b + 1])
                            last.then_inc(sem["a_v"], 1)

                        if mlp:
                            yield from keys_values()
                        yield
                        chan_norm(u, 1, CN, QA, "f_zT", "f_xn")
                        yield
                        kf = CK.rearrange("p h b t -> p (h b t)")
                        act.wait_ge(sem["f_k"], u.at("f_k", 1))
                        link(s.activation(kf, QB[:], ACT.Relu))
                        s.activation(kf, kf, ACT.Square).then_inc(sem["f_kk"], 1)
                        yield
                        act.wait_ge(sem["f_r"], u.at("f_r", 1))
                        s.activation(CR, QA[:], ACT.Tanh, scale=0.5).then_inc(sem["f_rr"], 1)
                        yield
                        norm_x(0)
                        if not mlp:
                            yield
                            for h in range(HALF):
                                act.wait_ge(sem["a_cT"], u.at("a_cT", h + 1))
                                s.activation(CT[:, h], bank(2 + h), ACT.Identity, bias=a_(u.layer, "ln_b")[:, h:h + 1],
                                             scale=a_(u.layer, "ln_w")[:, h:h + 1]).then_inc(sem["a_cc"], 1)
                            yield from keys_values()
                        def probs_out(n):
                            act.wait_ge(sem["a_pT"], u.at("a_pT", n + 1))
                            if n >= 2:
                                act.wait_ge(sem["a_pv"], u.at("a_pv", n - 1))
                            s.activation(PT[:, n % 2], bank(0).rearrange("p (j t) -> p j t", j=JH), ACT.Copy)\
                                .then_inc(sem["a_pc"], 1)

                        for n in range(JOBS):
                            yield
                            act.wait_ge(sem["a_max"], u.at("a_max", n + 1))
                            if n >= 2:
                                act.wait_ge(sem["a_pT"], u.at("a_pT", n - 1))
                            for j in range(JH):
                                last = s.activation(PR[:, n % 2, j], bank(2 + n % 2)[:, j * T:(j + 1) * T], ACT.Exp,
                                                    bias=nmax[:, n % 2, j:j + 1])
                            last.then_inc(sem["a_exp"], 1)
                            if n:
                                yield
                                probs_out(n - 1)
                        yield
                        probs_out(JOBS - 1)
                        yield
                        for h in range(HALF):
                            act.wait_ge(sem["a_oT"], u.at("a_oT", h + 1))
                            s.activation(CT[:, h], bank(2 + h), ACT.Copy).then_inc(sem["a_oc"], 1)
                        if mlp:
                            yield
                            norm_x(1)
                            for m in range(FFT):
                                yield
                                act.wait_ge(sem["a_fc"], u.at("a_fc", m + 1))
                                s.activation(H_[:, m], bank(m % 4), ACT.Gelu_apprx_tanh, bias=m_("fc_b")[:, m:m + 1])\
                                    .then_inc(sem["a_gelu"], 1)

                    for slot in slots:
                        in_order("ScalarE", slot, mixer, attn)

                @block.tensor
                def _(pe):
                    t = nc.tensor

                    def turn_tokens(dst, src, done):
                        for h in range(HALF):
                            for b in range(NB):
                                last = t.transpose(dst(h)[:, b * T:(b + 1) * T], src[:, b, h * P:(h + 1) * P], ident)
                            last.then_inc(done, 1)

                    def chan_proj(dst, w, src, done):
                        for m in range(HALF):
                            for h in range(HALF):
                                last = t.matmul(dst[:, m * 512:(m + 1) * 512], w[:, h, m * P:(m + 1) * P], src[:, h],
                                                start=(h == 0), stop=(h == HALF - 1))
                        last.then_inc(done, 1)

                    def add_bias(o, k):
                        return t.matmul(o, ones[0:BIASES, :], bias_rows(k), start=False, stop=True)

                    def token_proj(dst, w, lhs, done, bias=None):
                        for b in range(NB):
                            o = dst[:, b * C:(b + 1) * C]
                            for h in range(HALF):
                                last = t.matmul(o, lhs(h, b), w[:, h], start=(h == 0), stop=(h == HALF - 1 and bias is None))
                            if bias is not None:
                                last = add_bias(o, bias)
                        last.then_inc(done, 1)

                    def mixer(u):
                        L = u.layer
                        pa = lambda h: PA[:, h * 512:(h + 1) * 512]
                        pb = lambda h: PB[:, h * 512:(h + 1) * 512]
                        flat = lambda buf: buf[:].rearrange("p h b t -> p h (b t)")

                        def maa(f):
                            for h in range(HALF):
                                if f < 4:
                                    w2 = r_(L, "w2a")[MIX * f:MIX * f + MIX, h * P:(h + 1) * P]
                                    tt = TT[MIX * f:MIX * f + MIX, 0]
                                    pos = (MIX * f, 0)
                                else:
                                    w2 = r_(L, "w2b")[0:MIX, h * P:(h + 1) * P]
                                    tt = TT[0:MIX, 1]
                                    pos = (0, 0)
                                last = t.matmul(pa(h), w2, tt, start=True, stop=True, tile_position=pos)
                            last.then_inc(sem["r_maa"], 1)

                        yield
                        pe.wait_ge(sem["r_z"], u.at("r_z", 1))
                        turn_tokens(pa, z, sem["r_zT"])
                        yield
                        pe.wait_ge(sem["r_mixed"], u.at("r_mixed", 1))
                        w1 = rh_(L, "w1")
                        for h in range(HALF):
                            t.matmul(PB[:, 0:512], w1[:, h, 0:P], flat(X5[0])[:, h], start=(h == 0), stop=(h == 1))
                        for h in range(HALF):
                            last = t.matmul(PB[0:MIX, 512:1024], w1[:, h, P:P + MIX], flat(X5[0])[:, h], start=(h == 0), stop=(h == 1))
                        last.then_inc(sem["r_used"], 1)
                        yield
                        pe.wait_ge(sem["r_lowrank"], u.at("r_lowrank", 1))
                        maa(0)
                        yield
                        pe.wait_ge(sem["r_mixed"], u.at("r_mixed", 2))
                        maa(1)
                        yield
                        dw1 = rh_(L, "dw1")
                        for h in range(HALF):
                            last = t.matmul(PB[0:DEC, 0:512], dw1[:, h], flat(X5[1])[:, h], start=(h == 0), stop=(h == 1))
                        last.then_inc(sem["r_used"], 1)
                        yield
                        pe.wait_ge(sem["r_dec"], u.at("r_dec", 1))
                        for a in range(TB):
                            last = t.matmul(PB[:, a * C:(a + 1) * C],
                                            thT[0:DEC + 1, a * P:(a + 1) * P],
                                            r_(L, "dw2")[0:DEC + 1, :], start=True, stop=True)
                        last.then_inc(sem["r_decay"], 1)
                        for f, w in ((1, "Wk"), (2, "Wv"), (3, "Wr")):
                            yield
                            pe.wait_ge(sem["r_mixed"], u.at("r_mixed", f + 2))
                            maa(f + 1)
                            yield
                            pe.wait_ge(sem["r_turned"], u.at("r_turned", f))
                            src = flat(X5[(f + 1) % 2])
                            wt = rh_(L, w)
                            for a in range(TB):
                                for h in range(HALF):
                                    last = t.matmul(PB[:, a * C:(a + 1) * C], src[:, h, a * P:(a + 1) * P], wt[:, h],
                                                    start=(h == 0), stop=(h == HALF - 1))
                            last.then_inc(sem["r_used"], 1)
                        yield
                        pe.wait_ge(sem["r_mixed"], u.at("r_mixed", 6))
                        pe.wait_ge(sem["r_turned"], u.at("r_turned", 4))
                        wg = rh_(L, "Wg")
                        for m in range(HALF):
                            for h in range(HALF):
                                last = t.matmul(pb(m), wg[:, h, m * P:(m + 1) * P], flat(X5[1])[:, h], start=(h == 0), stop=(h == 1))
                        last.then_inc(sem["r_used"], 1)
                        yield
                        pe.wait_ge(sem["r_yt"], u.at("r_yt", 1))
                        yt = X5[1][:].rearrange("p h b t -> p (h b t)").rearrange("p (a c) -> p a c", a=TB)
                        turn_tokens(pb, yt, sem["r_yT"])
                        yield
                        pe.wait_ge(sem["r_yg"], u.at("r_yg", 1))
                        token_proj(PA, rh_(L, "Wo"), lambda h, b: SX[:, h, b], sem["r_o"])
                    def attn(u):
                        L = u.layer
                        mlp = u.kind == "attn_mlp"

                        def keys_values(c_t):
                            yield
                            if mlp:
                                pe.wait_ge(lane_sem["ld_ctx_t"][u.lane], 16)
                            else:
                                pe.wait_ge(sem["a_cc"], u.at("a_cc", 2))
                            for m in range(HALF):
                                for h in range(HALF):
                                    last = t.matmul(bank(2 + m), ah_(L, "Wk")[:, h, m * P:(m + 1) * P], c_t[:, h], start=(h == 0), stop=(h == 1))
                                last.then_inc(sem["a_kp"], 1)
                            yield
                            if not mlp:
                                pe.wait_ge(sem["a_q"], u.at("a_q", 2))
                            elif u.lane == 0:
                                pe.wait_ge(lane_sem["x_done"][1], u.other_x_done)
                            else:
                                pe.wait_ge(sem["a_out"], u.at("a_out", 0))
                            token_proj(QA, ah_(L, "Wv"), lambda h, b: c_t[:, h, b * T:(b + 1) * T], sem["a_vp"],
                                       0 if mlp else None)

                        if mlp:
                            yield from keys_values(ctx_chan[u.lane])
                        yield
                        if mlp:
                            pe.wait_ge(sem["a_v"], u.at("a_v", 1))
                        pe.wait_ge(sem["f_z"], u.at("f_z", 1))
                        turn_tokens(bank, az, sem["f_zT"])
                        yield
                        pe.wait_ge(sem["f_mixed"], u.at("f_mixed", 1))
                        chan_proj(QB, rh_(L, "fWk"), C5[0].rearrange("p h b t -> p h (b t)"), sem["f_k"])
                        yield
                        pe.wait_ge(sem["f_mixed"], u.at("f_mixed", 2))
                        token_proj(QA, rh_(L, "fWr"), lambda h, b: C5[1][:, h, b], sem["f_r"])
                        yield
                        pe.wait_ge(sem["f_kk"], u.at("f_kk", 1))
                        token_proj(QB, rh_(L, "fWv"), lambda h, b: CK[:, h, b], sem["f_v"])
                        yield
                        if mlp:
                            pe.wait_ge(sem["a_z"], u.at("a_z", 1))
                            turn_tokens(bank, az, sem["a_xT"])
                        else:
                            pe.wait_ge(lane_sem["x_done"][u.lane], u.at("x_done", 1))
                            turn_tokens(bank, X2[u.lane], sem["a_xT"])
                            yield
                            pe.wait_ge(sem["a_z"], u.at("a_z", 1))
                            turn_tokens(lambda h: bank(2 + h), az, sem["a_cT"])
                        yield
                        pe.wait_ge(sem["a_xc"], u.at("a_xc", 2))
                        for m in range(HALF):
                            for h in range(HALF):
                                last = t.matmul(bank(m), ah_(L, "Wq")[:, h, m * P:(m + 1) * P], XT[:, h], start=(h == 0), stop=(h == 1))
                            last.then_inc(sem["a_qp"], 1)
                        if not mlp:
                            yield from keys_values(CT[:])

                        def scores(n):
                            b, i = divmod(n, QUAD)
                            if n == 0:
                                pe.wait_ge(sem["a_q"], u.at("a_q", HALF))
                                pe.wait_ge(sem["a_k"], u.at("a_k", HALF))
                                if not mlp:
                                    pe.wait_ge(sem["a_mask"], u.at("a_mask", 1))
                            if n >= 2:
                                pe.wait_ge(sem["a_exp"], u.at("a_exp", n - 1))
                            rows = slice(32 * i, 32 * i + 32)
                            mask = mrow[u.lane][32 * i:32 * i + 1, b * T:(b + 1) * T].unsqueeze(1).broadcast_to([1, JH, T])
                            t.matmul(bank(2 + n % 2), ones[32 * i:32 * i + 1, :], mask, start=True, stop=False,
                                     tile_position=(32 * i, 0), skip_group_check=True)
                            for j in range(JH):
                                h, e = divmod(j, 2)
                                last = t.matmul(bank(2 + n % 2)[:, j * T:(j + 1) * T], Q_[rows, h, b * T:(b + 1) * T],
                                                K2[rows, e, h, b * T:(b + 1) * T], start=False, stop=True,
                                                tile_position=(32 * i, 0), skip_group_check=True)
                            last.then_inc(sem["a_s"], 1)

                        def probs_T(n):
                            pe.wait_ge(sem["a_exp"], u.at("a_exp", n + 1))
                            if n == 0:
                                pe.wait_ge(sem["a_v"], u.at("a_v", 1))
                            else:
                                pe.wait_ge(sem["a_pc"], u.at("a_pc", n))
                            for j in range(JH):
                                last = t.transpose(bank(0)[:, j * T:(j + 1) * T], PR[:, n % 2, j], ident)
                            last.then_inc(sem["a_pT"], 1)

                        def values(n):
                            b, i = divmod(n, QUAD)
                            pe.wait_ge(sem["a_pc"], u.at("a_pc", n + 1))
                            if n == 0:
                                pe.wait_ge(sem["a_vones"], u.at("a_vones", 1))
                            elif i == 0:
                                pe.wait_ge(sem["a_on"], u.at("a_on", b))
                            for j in range(JH):
                                h, e = divmod(j, 2)
                                head = 8 * h + 2 * i + e
                                last = t.matmul(bank(1)[:, head * (AD + 1):(head + 1) * (AD + 1)], PT[:, n % 2, j], VA[:, b, head],
                                                start=True, stop=True)
                            last.then_inc(sem["a_pv"], 1)

                        for n in range(JOBS + 2):
                            yield
                            if n < JOBS:
                                scores(n)
                            yield
                            if 1 <= n <= JOBS:
                                probs_T(n - 1)
                            if n >= 2:
                                values(n - 2)
                        yield
                        pe.wait_ge(sem["a_on"], u.at("a_on", NB))
                        turn_tokens(lambda h: bank(2 + h), az, sem["a_oT"])
                        yield
                        pe.wait_ge(sem["a_oc"], u.at("a_oc", 2))
                        token_proj(QA, ah_(L, "Wo"), lambda h, b: CT[:, h, b * T:(b + 1) * T], sem["a_o"],
                                   1 if mlp else None)
                        if mlp:
                            yield
                            pe.wait_ge(sem["a_z"], u.at("a_z", 2))
                            turn_tokens(lambda h: bank(2 + h), az, sem["a_xT"])
                            fc = m_("fc").rearrange("p (h n) -> p h n", h=HALF)
                            for m in range(FFT):
                                yield
                                if m == 0:
                                    pe.wait_ge(sem["a_xc"], u.at("a_xc", 4))
                                if m >= 4:
                                    pe.wait_ge(sem["a_gelu"], u.at("a_gelu", m - 3))
                                for h in range(HALF):
                                    last = t.matmul(bank(m % 4), fc[:, h, m * P:(m + 1) * P], XT[:, h], start=(h == 0), stop=(h == 1))
                                last.then_inc(sem["a_fc"], 1)
                            proj = m_("proj").rearrange("p (m n) -> p m n", m=FFT)
                            for b in range(NB):
                                yield
                                if b == 0:
                                    pe.wait_ge(sem["a_gelu"], u.at("a_gelu", FFT))
                                o = QA[:, b * C:(b + 1) * C]
                                for m in range(FFT):
                                    t.matmul(o, H_[:, m, b * T:(b + 1) * T], proj[:, m], start=(m == 0), stop=False)
                                last = add_bias(o, 2)
                            last.then_inc(sem["a_mlp"], 1)

                    for slot in slots:
                        in_order("TensorE", slot, mixer, attn)

        program([(mixing(0, 0, []),)], True, None)
        cleared = names + extra
        def clear():
            nc.all_engine_barrier()
            for n in cleared:
                nc.sync.sem_clear(sem[n])
            for pair in lane_sem.values():
                for one in pair:
                    nc.sync.sem_clear(one)
            nc.all_engine_barrier()

        with nc.Block() as block:
            @block.scalar
            def _(act):
                act.wait_ge(sem["loaded_w"], 80)
                nc.scalar.activation(tanh_gate[:], a_(0, "gate"), ACT.Tanh)

        clear()
        with nc.Fori(0, G // 2) as g:
            mixers, attentions = [], []
            for layer, lane in ((0, 1), (1, 0), (1, 1), (0, 0)):
                mixers.append((layer, lane))
            for layer, lane in ((0, 0), (0, 1), (1, 0), (1, 1)):
                attentions.append((layer, lane))
            done, slots = [], []
            for m, a in zip(mixers, attentions):
                slot = (mixing(*m, list(done)), attention(*a, list(done)))
                slots.append(slot)
                done += slot
            program(slots, False, g)
            clear()


def kernel(**inputs):
    import numpy as np
    import concourse.bacc as _bacc
    from concourse import mybir as _mybir
    from concourse.bass_utils import run_bass_kernel_spmd as _run

    a = {k: np.ascontiguousarray(v) for k, v in inputs.items()}
    perm = np.arange(C).reshape(RH, RS).T.reshape(-1)

    def vec(v):
        return v.reshape(-1, P).T

    def mat(w):
        return w.reshape(-1, P, w.shape[1]).transpose(1, 0, 2).reshape(P, -1)

    def rows(w):
        out = np.zeros((P, w.shape[1]), w.dtype)
        out[:w.shape[0]] = w
        return out

    def by_parity(b):
        out = np.zeros((2, HALF, P // 32, 2, AD), np.float32)
        heads = b.reshape(HALF, P // 32, 2, AD)
        for e in range(2):
            out[e, :, :, e] = heads[:, :, e]
        return out.reshape(2 * HALF, P).T

    def pack(cols, parts):
        for name, n in cols:
            assert parts[name].shape == (P, n), (name, parts[name].shape, n)
        return np.ascontiguousarray(np.concatenate([parts[name] for name, _ in cols], axis=1))

    def rwkv_pack(pre, order, maa, fk, fr, fwr, fwk, fwv):
        w = lambda n: a[f"{pre}_{n}"]
        w1 = w("maa_w1").reshape(C, NMIX, MIX)[:, order].reshape(C, NMIX * MIX)
        w2 = w("maa_w2")[order]
        dw2 = np.concatenate([w("decay_w2"), w("time_decay")[None]], 0)[:, perm]
        return pack(RWKV_COLS, dict(
            w1=mat(w1), w2a=w2[0:4].reshape(P, C), w2b=rows(w2[4]), dw1=mat(w("decay_w1")), dw2=rows(dw2),
            Wr=mat(w("Wr").T[:, perm]), Wk=mat(w("Wk").T[:, perm]), Wv=mat(w("Wv").T[:, perm]),
            Wg=mat(w("Wg").T[:, perm]), Wo=mat(w("Wo").T[perm]),
            fWr=mat(w(fwr).T), fWk=mat(w(fwk).T), fWv=mat(w(fwv).T),
            ln_w=np.concatenate([vec(w("ln1_w")), vec(w("ln2_w"))], 1),
            ln_b=np.concatenate([vec(w("ln1_b")), vec(w("ln2_b"))], 1),
            maa_x=vec(w("maa_x")), maa=np.concatenate([vec(m) for m in maa], 1),
            gn_w=vec(w("gn_w")[perm]), gn_b=vec(w("gn_b")[perm]), fk=vec(w(fk)), fr=vec(w(fr)),
            u=np.tile(w("faaaa").reshape(RH, RS), (NB, 1))))

    stack = a["L0_xattn_maa_stack"]
    r0 = rwkv_pack("L0_xattn", [1, 0, 2, 3, 4], [stack[i] for i in (1, 0, 2, 3, 4)], "ffn_maa_k", "ffn_maa_r",
                   "ffn_Wr", "ffn_Wk", "ffn_Wv")
    r1 = rwkv_pack("L2_xattn", [0, 1, 2, 3, 4], [a[f"L2_xattn_maa_{n}"] for n in "wkvrg"], "fmaa_k", "fmaa_r",
                   "fWr", "fWk", "fWv")
    zero4 = np.zeros((P, 2 * HALF), np.float32)
    w = lambda n: a[f"L1_xattn_{n}"]
    a0 = pack(ATTN_COLS, dict(
        Wq=mat(w("Wq").T), Wk=mat(w("Wk").T), Wv=mat(w("Wv").T), Wo=mat(w("Wo").T),
        qb=zero4[:, 0:HALF], kb=zero4,
        ln_w=np.concatenate([vec(w("ln_gamma")), zero4[:, 0:HALF]], 1),
        ln_b=np.concatenate([vec(w("ln_beta")), zero4[:, 0:HALF]], 1), gate=np.tile(w("gate")[None], (P, 1))))
    w3 = lambda n: a[f"L3_xattn_{n}"]
    a1 = pack(ATTN_COLS, dict(
        Wq=mat(w3("q_w")), Wk=mat(w3("k_w")), Wv=mat(w3("v_w")), Wo=mat(w3("cproj_w")),
        qb=vec(w3("q_b")), kb=by_parity(w3("k_b")),
        ln_w=np.concatenate([vec(w3("ln1_w")), vec(w3("ln2_w"))], 1),
        ln_b=np.concatenate([vec(w3("ln1_b")), vec(w3("ln2_b"))], 1), gate=zero4[:, 0:1]))
    mlp = pack(MLP_COLS, dict(fc=mat(w3("fc_w")), proj=mat(w3("proj_w")), fc_b=vec(w3("fc_b"))))
    parity = np.zeros((P // 32, 2, AD, 2), np.float32)
    parity[:, 0, :, 0] = parity[:, 1, :, 1] = 1.0
    common = pack(COMMON_COLS, dict(ident=np.eye(P, dtype=np.float32), parity=parity.reshape(P, 2)))

    ctx = a["ctx_2048"]
    mask = a["mask_BxS2_bf1"].view(np.uint8)
    again = lambda m: np.concatenate([m, m[0:1]])
    by_token = lambda m: m.reshape(G, NB, T, C).transpose(0, 2, 1, 3)
    arrays = {
        "x": again(by_token(a["x"])),
        "ctx": again(by_token(ctx)),
        "ctx_t": ctx.reshape(G, NB, T, HALF, P).transpose(0, 4, 3, 1, 2).reshape(G, P, HALF, N),
        "s0": again(ctx[:, 2:2 + RS].reshape(G, P, RS, RS)),
        "state": again(ctx[:, 0:2].reshape(G, NB, 2, HALF, P).transpose(0, 4, 2, 3, 1)),
        "mask_row": np.broadcast_to(mask.reshape(G, 1, N), (G, P, N)),
        "mask_col": mask.reshape(G, NB, T).transpose(0, 2, 1),
        "rwkv_w": np.stack([r0, r1]),
        "attn_w": np.stack([a0, a1]),
        "mlp_w": mlp,
        "bias_w": np.concatenate([w3("v_b"), w3("cproj_b"), w3("proj_b")])[None],
        "common": common,
    }
    arrays = {k: np.ascontiguousarray(v) for k, v in arrays.items()}
    nc = _bacc.Bacc("TRN2", target_bir_lowering=False, num_devices=1)
    args = [nc.dram_tensor(f"in_{k}", v.shape, _mybir.dt.from_np(v.dtype), kind="ExternalInput").ap() for k, v in arrays.items()]
    args.append(nc.dram_tensor("out_0", (G, T, NB, C), F32, kind="ExternalOutput").ap())
    build(nc, *args)
    r = _run(nc, [{f"in_{k}": v for k, v in arrays.items()}], core_ids=[0])
    return r.results[0]["out_0"].reshape(G, T, NB, C).transpose(0, 2, 1, 3).reshape(B, T, C)
```
